# Optimizing a Trainium2 kernel written in Bass

```python
import numpy as np
import jax
import jax.numpy as jnp

def _softmax(x, axis=-1):
    return jax.nn.softmax(x, axis=axis)

def _gelu(x):
    return jax.nn.gelu(x, approximate=True)

def _silu(x):
    return jax.nn.silu(x)

def _sigmoid(x):
    return jax.nn.sigmoid(x)

def _layernorm(x, axis=-1, eps=1e-05):
    m = jnp.mean(x, axis=axis, keepdims=True)
    v = jnp.var(x, axis=axis, keepdims=True)
    return (x - m) / jnp.sqrt(v + eps)

def _scatter_add(tgt, idx, src, axis=0):
    return tgt.at[idx].add(src)

def _segment_sum(src, seg, n):
    return jax.ops.segment_sum(src, seg, n)
kernel_name = 'mk_seq_preln_d1_jaxref_r8_71c5eb'

def setup_inputs(seed: int=0):
    np.random.seed(seed)
    _w = jnp.asarray

    def _L0_attn_setup():
        import jax, jax.numpy as jnp
        import numpy as np
        import math
        B, L, HID = (2, 512, 128)
        NH, DK, DV = (12, 64, 128)
        KD, VD, CS = (NH * DK, NH * DV, 4)
        SCALE = DK ** (-0.5)

        def _causal_depthwise_conv(x, w):
            c, k = w.shape
            xt = jnp.transpose(x, (0, 2, 1))
            out = jax.lax.conv_general_dilated(xt, w[:, None, :], window_strides=(1,), padding=[(k - 1, 0)], feature_group_count=c, dimension_numbers=('NCH', 'OIH', 'NCH'))
            return jnp.transpose(out, (0, 2, 1))

        def _l2norm(x, eps=1e-06):
            return x * jax.lax.rsqrt(jnp.sum(x * x, axis=-1, keepdims=True) + eps)

        def _gated_delta_net(hidden_states, Wq, Wk, Wv, Wg, Wo, conv_q, conv_k, conv_v, Wgk, Wb, b_b, A_log, dt_bias, g_norm_weight):
            b, l, _ = hidden_states.shape
            q = jax.nn.silu(_causal_depthwise_conv(hidden_states @ Wq, conv_q))
            k = jax.nn.silu(_causal_depthwise_conv(hidden_states @ Wk, conv_k))
            v = jax.nn.silu(_causal_depthwise_conv(hidden_states @ Wv, conv_v))
            gk = -jnp.exp(A_log) * jax.nn.softplus(hidden_states @ Wgk + dt_bias)
            beta = jax.nn.sigmoid(hidden_states @ Wb + b_b)
            q = jnp.transpose(q.reshape(b, l, NH, DK), (0, 2, 1, 3))
            k = jnp.transpose(k.reshape(b, l, NH, DK), (0, 2, 1, 3))
            v = jnp.transpose(v.reshape(b, l, NH, DV), (0, 2, 1, 3))
            q = _l2norm(q) * SCALE
            k = _l2norm(k)
            qs = jnp.moveaxis(q, 2, 0)
            ks_ = jnp.moveaxis(k, 2, 0)
            vs = jnp.moveaxis(v, 2, 0)
            bs = jnp.moveaxis(beta, 1, 0)
            gs = jnp.moveaxis(gk, 1, 0)

            def step(S, inp):
                qt, kt, vt, bt, gt = inp
                S = S * jnp.exp(gt)[..., None, None]
                kv = jnp.einsum('bhk,bhkv->bhv', kt, S)
                delta = (vt - kv) * bt[..., None]
                S = S + jnp.einsum('bhk,bhv->bhkv', kt, delta)
                ot = jnp.einsum('bhk,bhkv->bhv', qt, S)
                return (S, ot)
            S0 = jnp.zeros((b, NH, DK, DV), hidden_states.dtype)
            _, os_ = jax.lax.scan(step, S0, (qs, ks_, vs, bs, gs))
            o = jnp.moveaxis(os_, 0, 1)
            g = (hidden_states @ Wg).reshape(b, l, NH, DV)
            var = jnp.mean(o * o, axis=-1, keepdims=True)
            o = o * jax.lax.rsqrt(var + 1e-05) * g_norm_weight
            o = o * g * jax.nn.sigmoid(g)
            return o.reshape(b, l, VD) @ Wo
        key = jax.random.key(seed)
        ks = jax.random.split(key, 16)
        rn = lambda i, shape, s: jax.random.normal(ks[i], shape, jnp.float32) * s
        hidden_states = rn(0, (B, L, HID), 1.0)
        Wq = rn(1, (HID, KD), HID ** (-0.5))
        Wk = rn(2, (HID, KD), HID ** (-0.5))
        Wv = rn(3, (HID, VD), HID ** (-0.5))
        Wg = rn(4, (HID, VD), HID ** (-0.5))
        Wo = rn(5, (VD, HID), VD ** (-0.5))
        conv_q = rn(6, (KD, CS), 0.5)
        conv_k = rn(7, (KD, CS), 0.5)
        conv_v = rn(8, (VD, CS), 0.5)
        Wgk = rn(9, (HID, NH), HID ** (-0.5))
        Wb = rn(10, (HID, NH), HID ** (-0.5))
        b_b = rn(11, (NH,), 0.1)
        A = jax.random.uniform(ks[12], (NH,), jnp.float32, 0.5, 16.0)
        A_log = jnp.log(A)
        dt = jnp.exp(jax.random.uniform(ks[13], (NH,), jnp.float32) * (math.log(0.1) - math.log(0.001)) + math.log(0.001))
        dt = jnp.clip(dt, 0.0001, None)
        dt_bias = dt + jnp.log(-jnp.expm1(-dt))
        g_norm_weight = jnp.ones((DV,), jnp.float32)
        return dict(hidden_states=hidden_states, Wq=Wq, Wk=Wk, Wv=Wv, Wg=Wg, Wo=Wo, conv_q=conv_q, conv_k=conv_k, conv_v=conv_v, Wgk=Wgk, Wb=Wb, b_b=b_b, A_log=A_log, dt_bias=dt_bias, g_norm_weight=g_norm_weight)
    _L0_attn_in = _L0_attn_setup()

    def _L0_ffn_setup():
        import jax, jax.numpy as jnp
        import numpy as np
        DIM = 128
        DEPTH = 6
        HEADS = 16
        DIM_HEAD = 64
        WINDOW = 32
        INNER = HEADS * DIM_HEAD
        DIM_INNER = int(DIM * 4 * 2 / 3)
        QK_SCALE = 8.0

        def shift_tokens(t):
            a, s = jnp.split(t, 2, -1)
            s = jnp.pad(s, ((0, 0), (1, 0), (0, 0)))[:, :-1]
            return jnp.concatenate([a, s], -1)

        def l2norm(t):
            return t / jnp.maximum(jnp.linalg.norm(t, axis=-1, keepdims=True), 1e-12)

        def rotate_half(x):
            x1, x2 = jnp.split(x, 2, -1)
            return jnp.concatenate([-x2, x1], -1)

        def rotary_tables(n):
            half = jnp.arange(0, DIM_HEAD, 2, dtype=jnp.float32)
            inv_freq = 1.0 / 10000.0 ** (half / DIM_HEAD)
            t = jnp.arange(n, dtype=jnp.float32)
            freqs = t[:, None] * inv_freq[None, :]
            freqs = jnp.concatenate([freqs, freqs], -1)
            base_scale = (half + 0.4 * DIM_HEAD) / (1.4 * DIM_HEAD)
            power = (t - n // 2) / (WINDOW // 2)
            scale = base_scale[None, :] ** power[:, None]
            scale = jnp.concatenate([scale, scale], -1)
            return (freqs, scale)

        def local_attention(q, k, v):
            b, h, n, d = q.shape
            w = WINDOW
            nw = n // w
            bq = q.reshape(b, h, nw, w, d)
            bk = k.reshape(b, h, nw, w, d)
            bv = v.reshape(b, h, nw, w, d)

            def look(t):
                p = jnp.pad(t, ((0, 0), (0, 0), (1, 0), (0, 0), (0, 0)))
                return jnp.concatenate([p[:, :, :nw], p[:, :, 1:]], axis=3)
            bk2, bv2 = (look(bk), look(bv))
            seq = jnp.arange(n).reshape(nw, w)
            seq_p = jnp.pad(seq, ((1, 0), (0, 0)), constant_values=-1)
            jt = jnp.concatenate([seq_p[:nw], seq_p[1:]], axis=1)
            it = seq[:, :, None]
            jb = jt[:, None, :]
            mask = (it < jb) | (it > jb + w) | (jb == -1)
            sim = jnp.einsum('bhwie,bhwje->bhwij', bq, bk2) * QK_SCALE
            sim = jnp.where(mask, -jnp.finfo(sim.dtype).max, sim)
            attn = jax.nn.softmax(sim, -1)
            out = jnp.einsum('bhwij,bhwje->bhwie', attn, bv2)
            return out.reshape(b, h, n, d)

        def attn_layer(x, Wqkv, qs, ksc, Wo):
            b, n, _ = x.shape
            qkv = x @ Wqkv
            q, k, v = jnp.split(qkv, 3, -1)
            sh = lambda t: t.reshape(b, n, HEADS, DIM_HEAD).transpose(0, 2, 1, 3)
            q, k, v = (sh(q), sh(k), sh(v))
            q = l2norm(q) * qs
            k = l2norm(k) * ksc
            freqs, scale = rotary_tables(n)
            cos, sin = (jnp.cos(freqs), jnp.sin(freqs))
            q = q * cos * scale + rotate_half(q) * sin * scale
            inv = 1.0 / scale
            k = k * cos * inv + rotate_half(k) * sin * inv
            out = local_attention(q, k, v)
            out = out.transpose(0, 2, 1, 3).reshape(b, n, INNER)
            return out @ Wo

        def ffn_layer(x, g, bln, W1, b1, W2, b2):
            mu = x.mean(-1, keepdims=True)
            var = ((x - mu) ** 2).mean(-1, keepdims=True)
            xn = (x - mu) / jnp.sqrt(var + 1e-05) * g + bln
            hg = xn @ W1 + b1
            a, gate = jnp.split(hg, 2, -1)
            return a * jax.nn.gelu(gate, approximate=False) @ W2 + b2
        key = jax.random.key(seed)
        ks = jax.random.split(key, 8)
        B, N = (2, 256)
        init = lambda k, shape: jax.random.normal(k, shape, jnp.float32) * 0.02
        return {'x': jax.random.normal(ks[0], (B, N, DIM), jnp.float32), 'Wqkv': init(ks[1], (DEPTH, DIM, 3 * INNER)), 'q_scale': jnp.ones((DEPTH, DIM_HEAD), jnp.float32), 'k_scale': jnp.ones((DEPTH, DIM_HEAD), jnp.float32), 'Wo': init(ks[2], (DEPTH, INNER, DIM)), 'ln_g': jnp.ones((DEPTH, DIM), jnp.float32), 'ln_b': jnp.zeros((DEPTH, DIM), jnp.float32), 'W1': init(ks[3], (DEPTH, DIM, 2 * DIM_INNER)), 'b1': jnp.zeros((DEPTH, 2 * DIM_INNER), jnp.float32), 'W2': init(ks[4], (DEPTH, DIM_INNER, DIM)), 'b2': jnp.zeros((DEPTH, DIM), jnp.float32)}
    _L0_ffn_in = _L0_ffn_setup()
    _d = {'L0_attn_hidden_states': _L0_attn_in['hidden_states'], 'L0_attn_Wq': _L0_attn_in['Wq'], 'L0_attn_Wk': _L0_attn_in['Wk'], 'L0_attn_Wv': _L0_attn_in['Wv'], 'L0_attn_Wg': _L0_attn_in['Wg'], 'L0_attn_Wo': _L0_attn_in['Wo'], 'L0_attn_conv_q': _L0_attn_in['conv_q'], 'L0_attn_conv_k': _L0_attn_in['conv_k'], 'L0_attn_conv_v': _L0_attn_in['conv_v'], 'L0_attn_Wgk': _L0_attn_in['Wgk'], 'L0_attn_Wb': _L0_attn_in['Wb'], 'L0_attn_b_b': _L0_attn_in['b_b'], 'L0_attn_A_log': _L0_attn_in['A_log'], 'L0_attn_dt_bias': _L0_attn_in['dt_bias'], 'L0_attn_g_norm_weight': _L0_attn_in['g_norm_weight'], 'L0_ffn_Wqkv': _L0_ffn_in['Wqkv'], 'L0_ffn_q_scale': _L0_ffn_in['q_scale'], 'L0_ffn_k_scale': _L0_ffn_in['k_scale'], 'L0_ffn_Wo': _L0_ffn_in['Wo'], 'L0_ffn_ln_g': _L0_ffn_in['ln_g'], 'L0_ffn_ln_b': _L0_ffn_in['ln_b'], 'L0_ffn_W1': _L0_ffn_in['W1'], 'L0_ffn_b1': _L0_ffn_in['b1'], 'L0_ffn_W2': _L0_ffn_in['W2'], 'L0_ffn_b2': _L0_ffn_in['b2']}
    _x0 = _d['L0_attn_hidden_states']
    _d['L0_attn_hidden_states'] = jax.random.normal(jax.random.fold_in(jax.random.key(seed), 1), (8, 512, 128), dtype=_x0.dtype)
    del _x0
    return _d

def reference(L0_attn_hidden_states, L0_attn_Wq, L0_attn_Wk, L0_attn_Wv, L0_attn_Wg, L0_attn_Wo, L0_attn_conv_q, L0_attn_conv_k, L0_attn_conv_v, L0_attn_Wgk, L0_attn_Wb, L0_attn_b_b, L0_attn_A_log, L0_attn_dt_bias, L0_attn_g_norm_weight, L0_ffn_Wqkv, L0_ffn_q_scale, L0_ffn_k_scale, L0_ffn_Wo, L0_ffn_ln_g, L0_ffn_ln_b, L0_ffn_W1, L0_ffn_b1, L0_ffn_W2, L0_ffn_b2):

    def _L0_attn_ref(hidden_states, Wq, Wk, Wv, Wg, Wo, conv_q, conv_k, conv_v, Wgk, Wb, b_b, A_log, dt_bias, g_norm_weight):
        import jax, jax.numpy as jnp
        import numpy as np
        import math
        B, L, HID = (2, 512, 128)
        NH, DK, DV = (12, 64, 128)
        KD, VD, CS = (NH * DK, NH * DV, 4)
        SCALE = DK ** (-0.5)

        def _causal_depthwise_conv(x, w):
            c, k = w.shape
            xt = jnp.transpose(x, (0, 2, 1))
            out = jax.lax.conv_general_dilated(xt, w[:, None, :], window_strides=(1,), padding=[(k - 1, 0)], feature_group_count=c, dimension_numbers=('NCH', 'OIH', 'NCH'))
            return jnp.transpose(out, (0, 2, 1))

        def _l2norm(x, eps=1e-06):
            return x * jax.lax.rsqrt(jnp.sum(x * x, axis=-1, keepdims=True) + eps)

        def _gated_delta_net(hidden_states, Wq, Wk, Wv, Wg, Wo, conv_q, conv_k, conv_v, Wgk, Wb, b_b, A_log, dt_bias, g_norm_weight):
            b, l, _ = hidden_states.shape
            q = jax.nn.silu(_causal_depthwise_conv(hidden_states @ Wq, conv_q))
            k = jax.nn.silu(_causal_depthwise_conv(hidden_states @ Wk, conv_k))
            v = jax.nn.silu(_causal_depthwise_conv(hidden_states @ Wv, conv_v))
            gk = -jnp.exp(A_log) * jax.nn.softplus(hidden_states @ Wgk + dt_bias)
            beta = jax.nn.sigmoid(hidden_states @ Wb + b_b)
            q = jnp.transpose(q.reshape(b, l, NH, DK), (0, 2, 1, 3))
            k = jnp.transpose(k.reshape(b, l, NH, DK), (0, 2, 1, 3))
            v = jnp.transpose(v.reshape(b, l, NH, DV), (0, 2, 1, 3))
            q = _l2norm(q) * SCALE
            k = _l2norm(k)
            qs = jnp.moveaxis(q, 2, 0)
            ks_ = jnp.moveaxis(k, 2, 0)
            vs = jnp.moveaxis(v, 2, 0)
            bs = jnp.moveaxis(beta, 1, 0)
            gs = jnp.moveaxis(gk, 1, 0)

            def step(S, inp):
                qt, kt, vt, bt, gt = inp
                S = S * jnp.exp(gt)[..., None, None]
                kv = jnp.einsum('bhk,bhkv->bhv', kt, S)
                delta = (vt - kv) * bt[..., None]
                S = S + jnp.einsum('bhk,bhv->bhkv', kt, delta)
                ot = jnp.einsum('bhk,bhkv->bhv', qt, S)
                return (S, ot)
            S0 = jnp.zeros((b, NH, DK, DV), hidden_states.dtype)
            _, os_ = jax.lax.scan(step, S0, (qs, ks_, vs, bs, gs))
            o = jnp.moveaxis(os_, 0, 1)
            g = (hidden_states @ Wg).reshape(b, l, NH, DV)
            var = jnp.mean(o * o, axis=-1, keepdims=True)
            o = o * jax.lax.rsqrt(var + 1e-05) * g_norm_weight
            o = o * g * jax.nn.sigmoid(g)
            return o.reshape(b, l, VD) @ Wo
        return _gated_delta_net(hidden_states, Wq, Wk, Wv, Wg, Wo, conv_q, conv_k, conv_v, Wgk, Wb, b_b, A_log, dt_bias, g_norm_weight)

    def _L0_ffn_ref(x, Wqkv, q_scale, k_scale, Wo, ln_g, ln_b, W1, b1, W2, b2):
        import jax, jax.numpy as jnp
        import numpy as np
        DIM = 128
        DEPTH = 6
        HEADS = 16
        DIM_HEAD = 64
        WINDOW = 32
        INNER = HEADS * DIM_HEAD
        DIM_INNER = int(DIM * 4 * 2 / 3)
        QK_SCALE = 8.0

        def shift_tokens(t):
            a, s = jnp.split(t, 2, -1)
            s = jnp.pad(s, ((0, 0), (1, 0), (0, 0)))[:, :-1]
            return jnp.concatenate([a, s], -1)

        def l2norm(t):
            return t / jnp.maximum(jnp.linalg.norm(t, axis=-1, keepdims=True), 1e-12)

        def rotate_half(x):
            x1, x2 = jnp.split(x, 2, -1)
            return jnp.concatenate([-x2, x1], -1)

        def rotary_tables(n):
            half = jnp.arange(0, DIM_HEAD, 2, dtype=jnp.float32)
            inv_freq = 1.0 / 10000.0 ** (half / DIM_HEAD)
            t = jnp.arange(n, dtype=jnp.float32)
            freqs = t[:, None] * inv_freq[None, :]
            freqs = jnp.concatenate([freqs, freqs], -1)
            base_scale = (half + 0.4 * DIM_HEAD) / (1.4 * DIM_HEAD)
            power = (t - n // 2) / (WINDOW // 2)
            scale = base_scale[None, :] ** power[:, None]
            scale = jnp.concatenate([scale, scale], -1)
            return (freqs, scale)

        def local_attention(q, k, v):
            b, h, n, d = q.shape
            w = WINDOW
            nw = n // w
            bq = q.reshape(b, h, nw, w, d)
            bk = k.reshape(b, h, nw, w, d)
            bv = v.reshape(b, h, nw, w, d)

            def look(t):
                p = jnp.pad(t, ((0, 0), (0, 0), (1, 0), (0, 0), (0, 0)))
                return jnp.concatenate([p[:, :, :nw], p[:, :, 1:]], axis=3)
            bk2, bv2 = (look(bk), look(bv))
            seq = jnp.arange(n).reshape(nw, w)
            seq_p = jnp.pad(seq, ((1, 0), (0, 0)), constant_values=-1)
            jt = jnp.concatenate([seq_p[:nw], seq_p[1:]], axis=1)
            it = seq[:, :, None]
            jb = jt[:, None, :]
            mask = (it < jb) | (it > jb + w) | (jb == -1)
            sim = jnp.einsum('bhwie,bhwje->bhwij', bq, bk2) * QK_SCALE
            sim = jnp.where(mask, -jnp.finfo(sim.dtype).max, sim)
            attn = jax.nn.softmax(sim, -1)
            out = jnp.einsum('bhwij,bhwje->bhwie', attn, bv2)
            return out.reshape(b, h, n, d)

        def attn_layer(x, Wqkv, qs, ksc, Wo):
            b, n, _ = x.shape
            qkv = x @ Wqkv
            q, k, v = jnp.split(qkv, 3, -1)
            sh = lambda t: t.reshape(b, n, HEADS, DIM_HEAD).transpose(0, 2, 1, 3)
            q, k, v = (sh(q), sh(k), sh(v))
            q = l2norm(q) * qs
            k = l2norm(k) * ksc
            freqs, scale = rotary_tables(n)
            cos, sin = (jnp.cos(freqs), jnp.sin(freqs))
            q = q * cos * scale + rotate_half(q) * sin * scale
            inv = 1.0 / scale
            k = k * cos * inv + rotate_half(k) * sin * inv
            out = local_attention(q, k, v)
            out = out.transpose(0, 2, 1, 3).reshape(b, n, INNER)
            return out @ Wo

        def ffn_layer(x, g, bln, W1, b1, W2, b2):
            mu = x.mean(-1, keepdims=True)
            var = ((x - mu) ** 2).mean(-1, keepdims=True)
            xn = (x - mu) / jnp.sqrt(var + 1e-05) * g + bln
            hg = xn @ W1 + b1
            a, gate = jnp.split(hg, 2, -1)
            return a * jax.nn.gelu(gate, approximate=False) @ W2 + b2
        for i in range(DEPTH):
            x = attn_layer(shift_tokens(x), Wqkv[i], q_scale[i], k_scale[i], Wo[i]) + x
            x = ffn_layer(shift_tokens(x), ln_g[i], ln_b[i], W1[i], b1[i], W2[i], b2[i]) + x
        return x
    x = L0_attn_hidden_states
    x = x + _L0_attn_ref(_layernorm(x, axis=-1), L0_attn_Wq, L0_attn_Wk, L0_attn_Wv, L0_attn_Wg, L0_attn_Wo, L0_attn_conv_q, L0_attn_conv_k, L0_attn_conv_v, L0_attn_Wgk, L0_attn_Wb, L0_attn_b_b, L0_attn_A_log, L0_attn_dt_bias, L0_attn_g_norm_weight)
    x = x + _L0_ffn_ref(_layernorm(x, axis=-1), L0_ffn_Wqkv, L0_ffn_q_scale, L0_ffn_k_scale, L0_ffn_Wo, L0_ffn_ln_g, L0_ffn_ln_b, L0_ffn_W1, L0_ffn_b1, L0_ffn_W2, L0_ffn_b2)
    return x

_drawn_inputs = setup_inputs


def setup_inputs(seed=0):
    import zlib

    import numpy as np

    out = dict(_drawn_inputs(seed))
    spreads = {'L0_attn_g_norm_weight': (1.0, 0.2),
     'L0_ffn_q_scale': (1.0, 0.6),
     'L0_ffn_k_scale': (1.0, 0.6),
     'L0_ffn_ln_g': (1.0, 0.6),
     'L0_ffn_ln_b': (0.0, 0.8),
     'L0_ffn_b1': (0.0, 0.8),
     'L0_ffn_b2': (0.0, 0.1)}
    factors = {'L0_attn_b_b': 8.0, 'L0_ffn_W1': 3.901, 'L0_ffn_W2': 3.832}
    for name, (base, spread) in spreads.items():
        noise = np.random.default_rng([zlib.crc32(name.encode()), seed]).standard_normal(out[name].shape)
        drawn = base * np.exp(spread * noise) if base else spread * noise
        out[name] = jnp.asarray(drawn.astype(out[name].dtype))
    for name, factor in factors.items():
        out[name] = (out[name] * factor).astype(out[name].dtype)
    return out
```

```python
from contextlib import ExitStack

import numpy as np

import concourse.bass as bass
from concourse import mybir

F32 = mybir.dt.float32
BF16 = mybir.dt.bfloat16
ALU = mybir.AluOpType
ACT = mybir.ActivationFunctionType
AX = mybir.AxisListType.X

P = 128
DIM = 128
NSEQ, SEQ = 8, 512
GH, GDK, GDV, TAPS = 12, 64, 128, 4
CHUNK = 64
NCHUNK = SEQ // CHUNK
NPAIR = NSEQ // 2
NTILE = NPAIR * NCHUNK
GRP = 4
NGRP = GH // GRP
LEVELS = 6
DEPTH, HEADS, DH, WIN = 6, 16, 64, 32
INNER = HEADS * DH
FF = int(DIM * 4 * 2 / 3)
FF_TILES = [(0, 128), (128, 128), (256, FF - 256)]
BLK = 128
NBLK = SEQ // BLK
HALF = 256
WPB = BLK // WIN
LN_EPS = 1e-5
MASKED = -1e30


def constants():
    i = np.arange(P)
    seq = i // CHUNK
    same = seq[:, None] == seq[None, :]
    row, col = i[:, None], i[None, :]
    c = {}
    c["ident"] = np.eye(P)
    c["centre"] = np.eye(P) - 1.0 / P
    c["mean"] = np.full((P, P), 1.0 / P)
    c["later"] = same & (row > col)
    c["upto"] = same & (row <= col)
    c["before"] = same & (row < col)
    c["seq0"] = np.repeat(seq[:, None] == 0, P, 1)
    c["seq1"] = np.repeat(seq[:, None] == 1, P, 1)
    for lv in range(LEVELS):
        c[f"level{lv}"] = (row >> (lv + 1) == col >> (lv + 1)) & ((col >> lv) & 1 == 1) & ((row >> lv) & 1 == 0)
    names = list(c)
    mats = np.stack([np.asarray(c[n], np.float32) for n in names], 1)
    half = np.arange(0, DH, 2, dtype=np.float32)
    inv_freq = (np.float32(1.0) / np.float32(10000.0) ** (half / np.float32(DH))).astype(np.float32)
    t = np.arange(SEQ, dtype=np.float32)
    freqs = (t[:, None] * inv_freq[None, :]).astype(np.float32)
    base = ((half + np.float32(0.4 * DH)) / np.float32(1.4 * DH)).astype(np.float32)
    power = (t - SEQ // 2) / np.float32(WIN // 2)
    scale = (base[None, :] ** power[:, None]).astype(np.float32)
    inv = np.float32(1.0) / scale
    cos, sin = np.cos(freqs), np.sin(freqs)
    rope = np.stack([np.concatenate([cos * scale, cos * scale], 1) * 8, np.concatenate([-sin * scale, sin * scale], 1) * 8,
                     np.concatenate([cos * inv, cos * inv], 1), np.concatenate([-sin * inv, sin * inv], 1)])
    rope = rope.reshape(4, NBLK, P, DH).transpose(2, 0, 1, 3).astype(np.float32)
    q = i % WIN
    j = np.arange(2 * WIN)
    ok = (j[None, :] >= q[:, None]) & (j[None, :] <= q[:, None] + WIN)
    first = ok & ~((i[:, None] < WIN) & (j[None, :] < WIN))
    mask = np.stack([np.where(first, 0, MASKED), np.where(ok, 0, MASKED)], 1).astype(np.float32)
    return names, mats, rope, mask


class Mark:

    def __init__(self, lane, value):
        self.lane, self.value = lane, value


class Lane:

    def __init__(self, sem, step=1):
        self.sem, self.step, self.count, self.queue, self.seen = sem, step, 0, [], {}

    def after(self, *marks):
        for m in marks:
            if m is not None and self.seen.get(id(m.lane), 0) < m.value:
                self.seen[id(m.lane)] = m.value
                self.queue.append(lambda e, m=m: e.wait_ge(m.lane.sem, m.value))

    def do(self, emit, signal=True):
        if not signal:
            self.queue.append(emit)
            return None
        self.count += self.step
        self.queue.append(lambda e: emit(e).then_inc(self.sem, self.step))
        return Mark(self, self.count)

    def now(self):
        return Mark(self, self.count)

    def play(self, engine):
        for emit in self.queue:
            emit(engine)


def weave(*streams):
    live = list(streams)
    while live:
        for s in list(live):
            try:
                next(s)
            except StopIteration:
                live.remove(s)


class Arena:

    def __init__(self, tensor, cols):
        self.t, self.cols, self.at = tensor, cols, 0

    def take(self, *shape):
        n = int(np.prod(shape))
        assert self.at + n <= self.cols, (self.at, n, self.cols)
        v = self.t[:, self.at:self.at + n]
        self.at += n
        if len(shape) == 1:
            return v
        names = "abcd"[:len(shape)]
        return v.rearrange(f"p ({' '.join(names)}) -> p {' '.join(names)}", **dict(zip(names, shape)))


def build(nc, dram, out, names, nseq=NSEQ, depth=DEPTH):
    ctx = ExitStack()
    with ctx:
        def sem(name):
            return ctx.enter_context(nc.semaphore(name))

        pe, act, dve, pool = Lane(sem("s_pe")), Lane(sem("s_act")), Lane(sem("s_dve")), Lane(sem("s_pool"))
        sp = Lane(sem("s_sp"), 16)
        loads = {}

        def load(name, dst, src, key):
            if key not in loads:
                loads[key] = Lane(sem("s_load_" + key), 16)
            lane = loads[key]
            lane.count += 16
            sp.queue.append(lambda e: e.dma_start(dst, src).then_inc(lane.sem, 16))
            return Mark(lane, lane.count)

        cols = 52900
        arena = Arena(ctx.enter_context(nc.sbuf_tensor("arena", [P, cols], F32)), cols)
        bf = ctx.enter_context(nc.sbuf_tensor("bf", [P, 2 * 64 + P], BF16))
        psum = ctx.enter_context(nc.psum_tensor("banks", [P, 8, 512], F32))

        def mm(o, lhsT, rhs, start=True, stop=True, signal=False):
            return pe.do(lambda e: e.matmul(o, lhsT, rhs, start=start, stop=stop, skip_group_check=True), signal)

        def turn(o, i, signal=False):
            n = i.shape[0]
            return pe.do(lambda e: e.transpose(o, i, mat["ident"][0:n, 0:n]), signal)

        def tt(lane, o, a, b, op):
            return lane.do(lambda e: e.tensor_tensor(o, a, b, op))

        def ts(lane, o, a, s1, op0, s2=None, op1=ALU.bypass):
            return lane.do(lambda e: e.tensor_scalar(o, a, s1, s2, op0, op1))

        def stt(o, a, s, b, op0, op1):
            return dve.do(lambda e: e.scalar_tensor_tensor(out=o, in0=a, scalar=s, in1=b, op0=op0, op1=op1))

        def fn(o, a, f, **kw):
            return act.do(lambda e: e.activation(o, a, f, **kw))

        def total(lane, o, a, op=ALU.add):
            return lane.do(lambda e: e.tensor_reduce(o, a, AX, op))

        def memset(lane, o, value):
            return lane.do(lambda e: e.memset(o, value))

        def copy(lane, o, a):
            return lane.do(lambda e: e.tensor_copy(o, a))

        def recip(o, a):
            return dve.do(lambda e: e.reciprocal(o, a))

        def store(o, a):
            return sp.do(lambda e: e.dma_start(o, a))

        def bc(ap, n):
            return ap.unsqueeze(len(ap.shape)).broadcast_to(list(ap.shape) + [n])

        def bc_at(ap, axis, n):
            v = ap.unsqueeze(axis)
            s = list(v.shape)
            s[axis] = n
            return v.broadcast_to(s)

        resid = arena.take(nseq, SEQ + 1)
        mats = arena.take(len(names), P)
        mat = {n: mats[:, i, :] for i, n in enumerate(names)}
        minus_half = arena.take(1)
        base_mark = arena.at
        l_mats = load("mats", mats, dram["c_mats"], "mats")
        m_mh = memset(pool, minus_half, -0.5)

        npair, ntile = nseq // 2, nseq // 2 * NCHUNK
        x1 = arena.take(nseq, SEQ)
        xn = arena.take(nseq, SEQ + TAPS - 1)
        w_taps = arena.take(TAPS, NGRP, 4 * 256)
        w_g = arena.take(NGRP, GRP * GDV)
        w_o = arena.take(GH, DIM)
        w_gate = arena.take(2 * GH)
        gate_bias = arena.take(2 * GH)
        one_row = arena.take(P)
        a_log = arena.take(GH)
        g_norm = arena.take(1)
        gk = arena.take(ntile, GH)
        qmul = arena.take(ntile, 2, GH)
        kmul = arena.take(ntile, 4, GH)
        chunk_decay = arena.take(2, ntile, GH // 2)
        phase1_streams = arena.at
        l_x = load("x", x1, dram["xT"], "x")
        raw = resid.rearrange("p s t -> p (s t)")
        l_g = [load("w", w_g, dram["Wg"].rearrange("c (g n) -> c g n", g=NGRP), "w1"),
               load("w", w_o, dram["Wo"].rearrange("(h d) n -> d h n", d=GDV), "w1"),
               load("w", w_gate[:, 0:GH], dram["Wgk"], "w1"),
               load("w", w_gate[:, GH:2 * GH], dram["Wb"], "w1"),
               load("w", gate_bias[0:1, 0:GH], dram["dt_bias"].unsqueeze(0), "w1"),
               load("w", gate_bias[0:1, GH:2 * GH], dram["b_b"].unsqueeze(0), "w1"),
               load("w", a_log, dram["A_log"].partition_broadcast(P), "w1"),
               load("w", g_norm, dram["g_norm_weight"].unsqueeze(1), "w1")][-1]

        taps = Arena(arena.t, arena.cols)
        taps.at = arena.at
        conv_rows = taps.take(2, 1536)
        w_raw = taps.take(2, 1536)
        parts = [("Wq", "conv_q", 0, 256), ("Wk", "conv_k", 256, 256), ("Wv", "conv_v", 512, 512)]
        m_tap, n_tap = [None, None], 0
        for wname, cname, off, width in parts:
            n = NGRP * width
            sp.after(*m_tap)
            l_raw = load("w", w_raw[:, 0, 0:n], dram[wname], "raw")
            for tap in range(TAPS):
                i = n_tap % 2
                sp.after(m_tap[i])
                l_row = load("w", conv_rows[:, i, 0:n], dram[cname + "T"][tap].partition_broadcast(P), f"row{i}")
                pool.after(l_row, l_raw)
                m_tap[i] = tt(pool, w_taps[:, tap, :, off:off + width], w_raw[:, 0, 0:n].rearrange("p (g n) -> p g n", g=NGRP),
                              conv_rows[:, i, 0:n].rearrange("p (g n) -> p g n", g=NGRP), ALU.mult)
                n_tap += 1
        m_taps = m_tap
        pool.after(l_g)
        m_wo = ts(pool, w_o, w_o, g_norm[:, 0:1], ALU.mult)
        m_one = memset(pool, one_row, 1.0)
        m_pad = memset(pool, xn[:, :, 0:TAPS - 1], 0.0)

        ln_tmp = taps.take(2, 2, SEQ)
        bank_free = [None] * 8

        def layernorm(src, dst, n, banks, tmp, tmp_free, more=()):
            bc_, bv = banks
            pe.after(bank_free[bc_], l_mats, *more)
            m_c = mm(psum[:, bc_, 0:n], mat["centre"], src, signal=True)
            act.after(m_c, tmp_free)
            m_sq = fn(tmp[:, 0, 0:n], psum[:, bc_, 0:n], ACT.Square)
            pe.after(m_sq, bank_free[bv])
            m_v = mm(psum[:, bv, 0:n], mat["mean"], tmp[:, 0, 0:n], signal=True)
            dve.after(m_v, tmp_free)
            m_e = ts(dve, tmp[:, 1, 0:n], psum[:, bv, 0:n], LN_EPS, ALU.add)
            bank_free[bv] = m_e
            return m_c, m_e

        def rsqrt_small(o, a, after, scale=None, eps_=None, floor=None):
            pool.after(m_mh, *after)
            if floor is not None:
                m = ts(pool, o, a, floor, ALU.max)
            elif scale is not None:
                m = ts(pool, o, a, scale, ALU.mult, eps_, ALU.add)
            else:
                m = ts(pool, o, a, eps_, ALU.add)
            pool.after(m)
            return tt(pool, o, o, minus_half[:, 0:1].broadcast_to(list(o.shape)) if len(o.shape) == 2 else
                      minus_half[:, 0:1].unsqueeze(2).broadcast_to(list(o.shape)), ALU.pow)


        def rstd(tmp, m_e, n):
            act.after(m_e)
            m_r = fn(tmp[:, 1, 0:n], tmp[:, 1, 0:n], ACT.Sqrt)
            dve.after(m_r)
            return recip(tmp[:, 1, 0:n], tmp[:, 1, 0:n])

        tmp_free = [None, None]
        m_xn = []
        for s in range(nseq):
            i = s % 2
            m_c, m_e = layernorm(x1[:, s, :], None, SEQ, (2 * i, 2 * i + 1), ln_tmp[:, i], tmp_free[i], (l_x,))
            m_r = rstd(ln_tmp[:, i], m_e, SEQ)
            dve.after(m_r)
            m = tt(dve, xn[:, s, TAPS - 1:], psum[:, 2 * i, :], ln_tmp[:, i, 1, :], ALU.mult)
            bank_free[2 * i] = m
            tmp_free[i] = m
            m_xn.append(m)

        gates = taps.take(ntile, 2 * GH)
        gabs = taps.take(ntile, GH)
        gb = psum[:, 4:6, :]
        pe.after(l_g, m_one, m_xn[-1])
        per = 512 // (2 * GH)
        assert ntile <= 2 * per
        slots = []
        for t in range(ntile):
            pr, c = divmod(t, NCHUNK)
            o = gb[:, t // per, (t % per) * 2 * GH:(t % per + 1) * 2 * GH]
            slots.append(o)
            mm(o, one_row[0:1, :], gate_bias[0:1, :], True, False)
            for q in range(2):
                m_g = mm(o[64 * q:64 * q + 64, :], xn[:, 2 * pr + q, TAPS - 1 + c * CHUNK:TAPS - 1 + (c + 1) * CHUNK], w_gate, False, q == 1,
                         signal=(t == ntile - 1 and q == 1))
        dve.after(m_g)
        n0 = min(per, ntile)
        m = tt(dve, gates[:, 0:n0, :], gb[:, 0, 0:n0 * 2 * GH].rearrange("p (t g) -> p t g", g=2 * GH),
               bc_at(bc_at(minus_half[:, 0:1], 2, 1), 1, 1).broadcast_to([P, n0, 2 * GH]), ALU.bypass) if False else \
            copy(dve, gates[:, 0:n0, :], gb[:, 0, 0:n0 * 2 * GH].rearrange("p (t g) -> p t g", g=2 * GH))
        if ntile > n0:
            m = copy(dve, gates[:, n0:ntile, :], gb[:, 1, 0:(ntile - n0) * 2 * GH].rearrange("p (t g) -> p t g", g=2 * GH))
        bank_free[4] = bank_free[5] = m
        z, beta_in = gates[:, :, 0:GH], gates[:, :, GH:2 * GH]
        beta = kmul[:, :, 1, :]
        act.after(m)
        m_b = fn(beta, beta_in, ACT.Sigmoid)
        m = fn(gabs, z, ACT.Abs)
        act.after(m)
        m = fn(gabs, gabs, ACT.Exp, scale=-1.0)
        act.after(l_g)
        m_a = fn(a_log, a_log, ACT.Exp)
        act.after(m)
        m = fn(gabs, gabs, ACT.Ln, bias=1.0)
        dve.after(m, m_a)
        m = stt(gabs, z, 0.0, gabs, ALU.max, ALU.add)
        dve.after(m)
        m_gk = stt(gk, gabs, -1.0, bc_at(a_log, 1, ntile), ALU.mult, ALU.mult)
        pe.after(m_gk, bank_free[4], bank_free[5], l_mats, *[bank_free[k] for k in range(8)])
        gk_all = gk.rearrange("p t h -> p (t h)")
        ng = ntile * GH
        mm(psum[:, 4, 0:ng], mat["upto"], gk_all)
        mm(psum[:, 5, 0:ng], mat["later"], gk_all)
        mm(psum[:, 6, 0:ng], mat["seq0"], gk_all)
        m_cum = mm(psum[:, 7, 0:ng], mat["seq1"], gk_all, signal=True)
        act.after(m_cum)
        bank = lambda b: psum[:, b, 0:ng].rearrange("p (t h) -> p t h", h=GH)
        eg, tail = qmul[:, :, 1, :], kmul[:, :, 3, :]
        m_eg = fn(eg, bank(4), ACT.Exp)
        m_tail = fn(tail, bank(5), ACT.Exp)
        for q in range(2):
            for par in range(2):
                src = psum[64 * par:64 * par + 64, 6 + q, 0:ng].rearrange("p (t h u) -> p t h u", u=2, h=GH // 2)[:, :, :, par]
                m_dec = fn(chunk_decay[64 * par:64 * par + 64, q], src, ACT.Exp)
        for b in range(4, 8):
            bank_free[b] = m_dec
        pool.after(m_eg, m_b)
        m = tt(pool, kmul[:, :, 2, :], beta, eg, ALU.mult)
        pool.after(m)
        m = ts(pool, qmul[:, :, 1, :], eg, GDK ** -0.5, ALU.mult)
        m = memset(pool, qmul[:, :, 0, :], GDK ** -0.5)
        m_mul = memset(pool, kmul[:, :, 0, :], 1.0)
        x1_mark = [m_xn[-1]]
        setup_done = [pool.now(), act.now(), dve.now(), pe.now()]
        for lane in (pe, act, dve, pool):
            lane.after(*[mk for mk in setup_done if mk.lane is not lane])
            if lane is not pe:
                lane.after(lane.now())

        resid_cols = nseq * (SEQ + 1)
        stream_cols = 7600

        def shifted(pr, c):
            v = xn[:, 2 * pr, c * CHUNK:c * CHUNK + 1]
            return bass.AP(tensor=v.tensor, offset=v.offset, ap=[list(v.ap[0]), [1, TAPS], [SEQ + TAPS - 1, 2], [1, CHUNK]])

        def delta_stream(grp):
            a = Arena(arena.t, resid_cols if grp == NGRP - 1 else arena.cols)
            a.at = 0 if grp == NGRP - 1 else arena.at + grp * stream_cols
            QK = a.take(2, GRP, GDK)
            V = a.take(GRP, GDV)
            SG = a.take(GRP, GDV)
            KV4 = a.take(4, GRP, GDK)
            QV2 = a.take(2, GRP, GDK)
            DT = a.take(GRP, P)
            PT = a.take(GRP, P)
            if grp == NGRP - 1:
                a = Arena(arena.t, arena.cols)
                a.at = arena.at + grp * stream_cols
            M = a.take(GRP, P)
            Y = a.take(GRP, P)
            RHS = a.take(GRP, GDV)
            CT = a.take(5, 2, P)
            S = a.take(2, 2, GDV)
            ss = a.take(2, GRP)
            so = a.take(GRP)
            cq = a.take(2, GRP)
            ck = a.take(4, GRP)
            matrix = lambda v: v.rearrange("p a h d -> p (a h d)").rearrange("p (r n) -> p r n", r=GRP)
            XT = PT
            NT = matrix(QK)
            T = matrix(KV4[:, 0:2])
            R = matrix(QV2)
            U = DT
            A, B = 2 * grp, 2 * grp + 1
            AB = psum[:, A:A + 2, :]
            b4 = lambda b: psum[:, b, :].rearrange("p (r n) -> p r n", r=GRP)
            free = {A: bank_free[A], B: bank_free[B]}
            heads = lambda ap, t: ap[:, t, grp * GRP:(grp + 1) * GRP]
            by_parity = lambda ap: ap.rearrange("p (h u) -> p u h", u=2)
            last = []
            for t in range(ntile):
                pr, c = divmod(t, NCHUNK)
                tok = lambda tap: XT[:, tap, :]
                for lane in (pe, act, dve, pool):
                    lane.after(*last)
                if c == 0:
                    m_S = memset(pool, S, 0.0)
                m_xt = copy(pool, XT.rearrange("p t (q n) -> p t q n", q=2), shifted(pr, c))
                pe.after(free[A], m_xt)
                for tap in range(TAPS):
                    m_qk = mm(psum[:, A, :], tok(tap), w_taps[:, tap, grp, 0:512], tap == 0, tap == TAPS - 1, signal=(tap == TAPS - 1))
                pe.after(free[B])
                act.after(m_qk)
                m_qk = fn(QK.rearrange("p a h d -> p (a h d)"), psum[:, A, :], ACT.Silu)
                free[A] = m_qk
                yield
                for tap in range(TAPS):
                    m_v = mm(psum[:, B, :], tok(tap), w_taps[:, tap, grp, 512:1024], tap == 0, tap == TAPS - 1, signal=(tap == TAPS - 1))
                m_ug = tt(pool, Y.rearrange("p (u h) n -> p u h n", u=2),
                          bc_at(bc_at(mat["later"], 1, 2), 1, 2), bc(by_parity(heads(gk, t)), P), ALU.mult)
                act.after(m_v)
                m_v = fn(V.rearrange("p h d -> p (h d)"), psum[:, B, :], ACT.Silu)
                free[B] = m_v
                pe.after(free[A])
                m_g = mm(psum[:, A, :], tok(TAPS - 1), w_g[:, grp, :], signal=True)
                act.after(m_g)
                m_sg = fn(SG.rearrange("p h d -> p (h d)"), psum[:, A, :], ACT.Silu)
                free[A] = m_sg
                pool.after(m_qk)
                m_sq = tt(pool, RHS.rearrange("p h d -> p (h d)"), QK.rearrange("p a h d -> p (a h d)"),
                          QK.rearrange("p a h d -> p (a h d)"), ALU.mult)
                pe.after(m_ug, free[B])
                for r in range(GRP):
                    m_dt = mm(b4(B)[:, r, :], Y[:, r, :], mat["upto"], signal=(r == GRP - 1))
                yield
                act.after(m_dt)
                m_dt = fn(DT, b4(B), ACT.Exp)
                free[B] = m_dt
                dve.after(m_sq)
                m_ss = total(dve, ss.rearrange("p a h -> p (a h)"), RHS.rearrange("p h d -> p (h d)").rearrange("p (x d) -> p x d", d=GDK))
                m_rn = rsqrt_small(ss.rearrange("p a h -> p (a h)"), ss.rearrange("p a h -> p (a h)"), (m_ss,), eps_=1e-6)
                pool.after(m_rn)
                m1 = tt(pool, cq, bc_at(ss[:, 0, :], 1, 2), qmul[:, t, :, grp * GRP:(grp + 1) * GRP], ALU.mult)
                m2 = tt(pool, ck, bc_at(ss[:, 1, :], 1, 4), kmul[:, t, :, grp * GRP:(grp + 1) * GRP], ALU.mult)
                dve.after(m2)
                m_k4 = tt(dve, KV4, bc_at(QK[:, 1], 1, 4), bc(ck, GDK), ALU.mult)
                m_q2 = tt(dve, QV2, bc_at(QK[:, 0], 1, 2), bc(cq, GDK), ALU.mult)
                yield
                pair = lambda v, hp: v[:, 2 * hp:2 * hp + 2, :].rearrange("p h d -> p (h d)")
                pe.after(m_q2, free[A], free[B])
                for f in range(2):
                    for hp in range(2):
                        turn(psum[:, A, (2 * f + hp) * P:(2 * f + hp + 1) * P], pair(KV4[:, f], hp))
                m_ta = turn(psum[:, B, 0:P], pair(QV2[:, 0], 0), True)
                turn(psum[:, B, P:2 * P], pair(QV2[:, 0], 1))
                turn(psum[:, B, 2 * P:3 * P], pair(QV2[:, 1], 0))
                m_tb = turn(psum[:, B, 3 * P:4 * P], pair(QV2[:, 1], 1), True)
                act.after(m_ta)
                m_c1 = fn(CT[:, 0:2].rearrange("p a b c -> p (a b c)"), psum[:, A, :], ACT.Copy)
                act.after(m_tb)
                m_c2 = fn(CT[:, 2:4].rearrange("p a b c -> p (a b c)"), psum[:, B, :], ACT.Copy)
                pe.after(m_c1)
                for hp in range(2):
                    m_tc = turn(psum[:, A, hp * P:(hp + 1) * P], pair(KV4[:, 2], hp), hp == 1)
                act.after(m_tc)
                m_c3 = fn(CT[:, 4].rearrange("p b c -> p (b c)"), psum[:, A, 0:2 * P], ACT.Copy)
                pool.after(m_dt)
                m_m = tt(pool, M, DT, bc_at(mat["before"], 1, GRP), ALU.mult)
                m_dp = tt(pool, DT, DT, bc_at(mat["upto"], 1, GRP), ALU.mult)
                m_vb = tt(pool, V, V, bc(heads(beta, t), GDV), ALU.mult)
                yield
                pe.after(m_c3)
                for par in range(2):
                    for hp in range(2):
                        rows = slice(64 * par, 64 * par + 64)
                        m_np = mm(AB[:, par, hp * 256:(hp + 1) * 256].rearrange("p (k n) -> p k n", k=2),
                                  CT[rows, 0, hp, :], CT[rows, 1:3, hp, :], signal=(par == 1 and hp == 1))
                dve.after(m_np, m_dp)
                prod = AB.rearrange("p u (h k n) -> p u h k n", h=2, k=2)
                m_nt = tt(dve, NT.rearrange("p (u h) n -> p u h n", u=2), prod[:, :, :, 0, :],
                          M.rearrange("p (u h) n -> p u h n", u=2), ALU.mult)
                m_pt = tt(dve, PT.rearrange("p (u h) n -> p u h n", u=2), prod[:, :, :, 1, :],
                          DT.rearrange("p (u h) n -> p u h n", u=2), ALU.mult)
                free[A] = free[B] = m_pt
                yield
                pool.after(m_nt)
                m_M = tt(pool, M, NT, bc_at(mat["level0"], 1, GRP), ALU.mult)
                pe.after(m_M, free[A])
                for r in range(GRP):
                    m_t = turn(b4(A)[:, r, :], M[:, r, :], r == GRP - 1)
                pool.after(m_M)
                m_R = tt(pool, R, bc_at(mat["ident"], 1, GRP), M, ALU.subtract)
                dve.after(m_t)
                m_T = tt(dve, T, bc_at(mat["ident"], 1, GRP), b4(A), ALU.subtract)
                free[A] = m_T
                pe.after(m_R)
                for lv in range(1, LEVELS):
                    pool.after(m_M, m_t, m_R if lv == 1 else None)
                    m_M = tt(pool, M, NT, bc_at(mat[f"level{lv}"], 1, GRP), ALU.mult)
                    pe.after(m_M, m_T, free[A])
                    for r in range(GRP):
                        m_y = mm(b4(A)[:, r, :], M[:, r, :], T[:, r, :], signal=(r == GRP - 1))
                    m_t = m_y
                    act.after(m_y)
                    m_y = fn(Y, b4(A), ACT.Copy)
                    free[A] = m_y
                    yield
                    pe.after(m_y, m_R, free[B])
                    if lv < LEVELS - 1:
                        for r in range(GRP):
                            m_z = mm(b4(B)[:, r, :], R[:, r, :], Y[:, r, :], signal=(r == GRP - 1))
                    for r in range(GRP):
                        m_w = mm(b4(A)[:, r, :], Y[:, r, :], R[:, r, :], signal=(r == GRP - 1))
                    if lv < LEVELS - 1:
                        dve.after(m_z)
                        m_T = tt(dve, T, T, b4(B), ALU.subtract)
                        free[B] = m_T
                    dve.after(m_w)
                    m_R = tt(dve, R, R, b4(A), ALU.subtract)
                    free[A] = m_R
                    yield
                pe.after(m_R, m_S)
                for hp in range(2):
                    for par in range(2):
                        rows = slice(64 * par, 64 * par + 64)
                        for q in range(2):
                            m_ks = mm(AB[64 * q:64 * q + 64, par, hp * GDV:(hp + 1) * GDV], CT[rows, 4, hp, 64 * q:64 * q + 64],
                                      S[rows, q, hp, :], signal=(hp == 1 and par == 1 and q == 1))
                dve.after(m_ks, m_vb)
                m_rhs = tt(dve, RHS.rearrange("p (u h) n -> p u h n", u=2), V.rearrange("p (h u) n -> p u h n", u=2),
                           AB[:, :, 0:2 * GDV].rearrange("p u (h n) -> p u h n", h=2), ALU.subtract)
                yield
                pe.after(m_rhs)
                for r in range(GRP):
                    m_u = mm(b4(A)[:, r, :], R[:, r, :], RHS[:, r, :], signal=(r == GRP - 1))
                act.after(m_u)
                m_u = fn(U, b4(A), ACT.Copy)
                yield
                pe.after(m_u)
                for hp in range(2):
                    for par in range(2):
                        rows = slice(64 * par, 64 * par + 64)
                        o = AB[:, par, hp * GDV:(hp + 1) * GDV]
                        mm(o, PT[:, 2 * par + hp, :], U[:, 2 * par + hp, :], True, False)
                        for q in range(2):
                            m_o = mm(o[64 * q:64 * q + 64, :], CT[rows, 3, hp, 64 * q:64 * q + 64], S[rows, q, hp, :],
                                     False, q == 1, signal=(hp == 1 and par == 1 and q == 1))
                O = AB[:, :, 0:2 * GDV].rearrange("p u (h n) -> p u h n", h=2)
                O2 = AB[:, :, 0:2 * GDV]
                act.after(m_o)
                m_sq = fn(Y.rearrange("p (u h) n -> p u (h n)", u=2), O2, ACT.Square)
                pool.after(m_o)
                m_S = tt(pool, S, S, bc(chunk_decay[:, :, t, grp * 2:grp * 2 + 2], GDV), ALU.mult)
                dve.after(m_sq)
                m_so = total(dve, so, Y)
                m_so = rsqrt_small(so, so, (m_so,), scale=1.0 / GDV, eps_=1e-5)
                dve.after(m_so)
                m_on = tt(dve, RHS.rearrange("p (u h) n -> p u h n", u=2), O,
                          bc(so.rearrange("p (u h) -> p u h", u=2), GDV), ALU.mult)
                pool.after(m_on)
                m_on2 = tt(pool, RHS.rearrange("p (u h) n -> p u h n", u=2), RHS.rearrange("p (u h) n -> p u h n", u=2),
                           SG.rearrange("p (h u) n -> p u h n", u=2), ALU.mult)
                yield
                pe.after(m_on)
                for hp in range(2):
                    for q in range(2):
                        rows = slice(64 * q, 64 * q + 64)
                        for par in range(2):
                            m_s = mm(AB[64 * par:64 * par + 64, q, hp * GDV:(hp + 1) * GDV], KV4[rows, 3, 2 * hp + par, :],
                                     U[rows, 2 * par + hp, :], signal=(hp == 1 and par == 1 and q == 1))
                dve.after(m_s, m_S)
                m_S = tt(dve, S, S, AB[:, :, 0:2 * GDV].rearrange("p u (h n) -> p u h n", h=2), ALU.add)
                pe.after(m_on2, m_S)
                for r in range(GRP):
                    m_ot = turn(b4(A)[:, r, :], RHS[:, r, :], r == GRP - 1)
                act.after(m_ot)
                m_ot = fn(Y, b4(A), ACT.Copy)
                yield
                pe.after(m_ot)
                for r in range(GRP):
                    h = grp * GRP + 2 * (r % 2) + r // 2
                    m_y = mm(psum[:, B, 0:P], w_o[:, h, :], Y[:, r, :], r == 0, r == GRP - 1, signal=(r == GRP - 1))
                dve.after(m_y, x1_mark[0])
                xs = x1[:, 2 * pr:2 * pr + 2, c * CHUNK:(c + 1) * CHUNK]
                m_x = tt(dve, xs, xs, psum[:, B, 0:P].rearrange("p (q n) -> p q n", q=2), ALU.add)
                x1_mark[0] = m_x
                free[A], free[B] = m_ot, m_x
                last = [pe.now(), act.now(), dve.now(), pool.now()]
                yield
            bank_free[A], bank_free[B] = free[A], free[B]

        weave(*[delta_stream(g) for g in range(NGRP)])

        phase_end = [pe.now(), act.now(), dve.now(), pool.now()]
        sp_store = None
        sp.after(*phase_end)
        m_park = store(out, x1)
        for lane in (pe, act, dve, pool):
            lane.after(*phase_end)

        def reset_bank_free():
            for b in range(8):
                bank_free[b] = None
        reset_bank_free()
        lt = Arena(arena.t, arena.cols)
        lt.at = xn_at = base_mark + nseq * SEQ
        ln_tmp = lt.take(2, 2, SEQ)
        m_z = memset(pool, resid[64:P, :, 0:1], 0.0)
        tmp_free = [None, None]
        for s in range(nseq):
            i = s % 2
            m_c, m_e = layernorm(x1[:, s, :], None, SEQ, (2 * i, 2 * i + 1), ln_tmp[:, i], tmp_free[i])
            m_r = rstd(ln_tmp[:, i], m_e, SEQ)
            dve.after(m_r)
            tt(dve, resid[0:64, s, 0:SEQ], psum[0:64, 2 * i, :], ln_tmp[0:64, i, 1, :], ALU.mult)
            m = tt(dve, resid[64:P, s, 1:SEQ + 1], psum[64:P, 2 * i, :], ln_tmp[64:P, i, 1, :], ALU.mult)
            bank_free[2 * i] = m
            tmp_free[i] = m
        m_resid0 = m
        phase_end = [pe.now(), act.now(), dve.now(), pool.now()]
        sp.after(*phase_end)
        sp.after(m_park)
        for lane in (pe, act, dve, pool):
            lane.after(*phase_end)
            lane.after(m_park)
        reset_bank_free()

        arena.at = base_mark
        rope0 = arena.take(4, NBLK, DH)
        rope = arena.take(4, NBLK, DH)
        qk_scale = arena.take(2, DH)
        w_qkv = arena.take(3 * INNER)
        w_out = arena.take(8, DIM)
        w1_raw = arena.take(2 * FF)
        w1 = arena.take(2 * FF)
        w2 = arena.take(3, DIM)
        ln_gb = arena.take(2)
        b1c = arena.take(6)
        b2c = arena.take(1)
        streams_at = arena.at
        stream_cols = (arena.cols - arena.at) // 2
        mask_bf = bf[:, 0:128].rearrange("p (k n) -> p k n", k=2)
        ident_bf = bf[:, 128:256]
        mask_f = w_qkv[:, 0:128].rearrange("p (k n) -> p k n", k=2)
        l_rope = load("rope", rope0, dram["c_rope"], "rope")
        l_mask = load("mask", mask_f, dram["c_mask"], "rope")
        pool.after(l_mask)
        m_maskbf = copy(pool, mask_bf, mask_f)
        m_idbf = copy(pool, ident_bf, mat["ident"])
        sp.after(m_idbf)
        for lane in (pe, act, dve):
            lane.after(m_idbf)

        layer_ready = {}
        layer_used = []

        def load_layer(ly):
            sp.after(*layer_used)
            k = "lw"
            load("w", qk_scale[:, 0, :], dram["q_scale"][ly].partition_broadcast(P), k)
            load("w", qk_scale[:, 1, :], dram["k_scale"][ly].partition_broadcast(P), k)
            load("w", w_qkv, dram["Wqkv"][ly], k)
            for e_ in range(2):
                for u in range(2):
                    load("w", w_out[64 * u:64 * u + 64, :, :].rearrange("p (e j) n -> p e j n", e=2)[:, e_],
                         dram["Wo2"][ly, (8 * e_ + 4 * u) * DH:(8 * e_ + 4 * u + 4) * DH, :].rearrange("(j d) n -> d j n", d=DH), k)
            load("w", w1_raw, dram["W1"][ly], k)
            for i, (r0, nr) in enumerate(FF_TILES):
                load("w", w2[0:nr, i, :], dram["W2"][ly, r0:r0 + nr, :], k)
                load("w", b1c[0:nr, i:i + 1], dram["b1"][ly, r0:r0 + nr].unsqueeze(1), k)
                load("w", b1c[0:nr, 3 + i:4 + i], dram["b1"][ly, FF + r0:FF + r0 + nr].unsqueeze(1), k)
            load("w", b2c, dram["b2"][ly].unsqueeze(1), k)
            load("w", ln_gb[:, 0:1], dram["ln_g"][ly].unsqueeze(1), k)
            l_w = load("w", ln_gb[:, 1:2], dram["ln_b"][ly].unsqueeze(1), k)
            pool.after(l_w, l_rope, *layer_used)
            for i in range(2):
                tt(pool, rope[:, 2 * i], rope0[:, 2 * i], bc_at(qk_scale[:, i, :], 1, NBLK), ALU.mult)
                for z in range(2):
                    lo, hi = slice(32 * z, 32 * z + 32), slice(32 * (1 - z), 32 * (1 - z) + 32)
                    tt(pool, rope[:, 2 * i + 1, :, lo], rope0[:, 2 * i + 1, :, lo], bc_at(qk_scale[:, i, hi], 1, NBLK), ALU.mult)
            m_w1 = ts(pool, w1, w1_raw, ln_gb[:, 0:1], ALU.mult)
            pe.after(l_w, *layer_used)
            for i in range(6):
                r0, nr = FF_TILES[i % 3]
                off = (i // 3) * FF + r0
                m_b = mm(psum[0:nr, 0, i:i + 1], w1_raw[:, off:off + nr], ln_gb[:, 1:2], signal=(i == 5))
            dve.after(m_b, l_w)
            for i in (0, 1, 2):
                nr = FF_TILES[i][1]
                m = tt(dve, b1c[0:nr, i:6:3], b1c[0:nr, i:6:3], psum[0:nr, 0, i:6:3], ALU.add)
            for lane in (pe, act, dve, pool):
                lane.after(m_w1, m, l_w)

        def layer_stream(i_stream, ly, seqs):
            a = Arena(arena.t, arena.cols)
            a.at = streams_at + i_stream * stream_cols
            SQ = a.take(HEADS, DH)
            QN = a.take(HEADS, DH)
            T1 = a.take(HEADS, DH)
            PR = a.take(2, HEADS, WIN)
            QT = a.take(8, HALF)
            KT = a.take(8, WIN + HALF)
            V4 = a.take(9, 4, DH)
            PT = a.take(4, 2, HALF)
            OT = a.take(8, HALF)
            stat = a.take(2, HEADS)
            mx = a.take(HEADS)
            sm = a.take(HEADS)
            assert a.at <= streams_at + (i_stream + 1) * stream_cols, a.at - (streams_at + (i_stream + 1) * stream_cols)
            f = Arena(arena.t, arena.cols)
            f.at = streams_at + i_stream * stream_cols
            LT = f.take(2, SEQ)
            XN = f.take(SEQ)
            G = f.take(3, SEQ // 2)
            H = f.take(3, SEQ // 2)
            assert f.at <= streams_at + i_stream * stream_cols + 4 * 1024 + 0
            base = 4 * i_stream
            free = {0: bank_free[base], 1: bank_free[base + 1], 2: bank_free[base + 2], 3: bank_free[base + 3]}
            bk = lambda k, n=1: psum[:, base + k:base + k + n, :]
            last = []
            for s in seqs:
                for lane in (pe, act, dve, pool):
                    lane.after(*last)
                xs = resid[:, s, 0:SEQ]
                memset(pool, KT[:, :, 0:WIN], 0.0)
                m_zero = memset(pool, V4[:, 0], 0.0)
                m_kt = m_v4 = m_avd = m_woq = m_h2 = None
                for half in range(2):
                    if half:
                        pool.after(m_avd, m_kt, m_sc, m_v4)
                        m1 = copy(pool, KT[:, :, 0:WIN], KT[:, :, HALF:HALF + WIN])
                        m_zero = copy(pool, V4[:, 0], V4[:, 8])
                        m_pt_read = m_avd
                    act.after(m_zero)
                    dve.after(m_zero)
                    for b2 in range(2):
                        b = 2 * half + b2
                        xb = xs[:, b * BLK:(b + 1) * BLK]
                        for i in range(2):
                            p0 = 2 * i
                            pe.after(free[p0], free[p0 + 1])
                            for n in range(2):
                                m_p = mm(bk(p0 + n)[:, 0, :], xb, w_qkv[:, i * INNER + n * 512:i * INNER + (n + 1) * 512], signal=(n == 1))
                            flat = bk(p0, 2).rearrange("p a n -> p (a n)")
                            hd = flat.rearrange("p (h d) -> p h d", d=DH)
                            act.after(m_p, dve.now())
                            m_sq = fn(SQ.rearrange("p h d -> p (h d)"), flat, ACT.Square)
                            dve.after(m_sq)
                            m_ss = total(dve, stat[:, i, :], SQ)
                            m_rn = rsqrt_small(stat[:, i, :], stat[:, i, :], (m_ss,), floor=1e-24)
                            dve.after(m_rn, pool.now())
                            m_qn = tt(dve, QN, hd, bc(stat[:, i, :], DH), ALU.mult)
                            free[p0] = free[p0 + 1] = m_qn
                            yield
                            pool.after(m_qn)
                            for z in range(2):
                                lo, hi = slice(32 * z, 32 * z + 32), slice(32 * (1 - z), 32 * (1 - z) + 32)
                                m_t2 = tt(pool, SQ[:, :, lo], QN[:, :, hi], bc_at(rope[:, 2 * i + 1, b, lo], 1, HEADS), ALU.mult)
                            dve.after(m_qn, pe.now())
                            m_t1 = tt(dve, T1, QN, bc_at(rope[:, 2 * i, b, :], 1, HEADS), ALU.mult)
                            dve.after(m_t1, m_t2)
                            m_t1 = tt(dve, T1, T1, SQ, ALU.add)
                            yield
                            pe.after(m_t1, free[p0], free[p0 + 1])
                            for hp in range(8):
                                m_tt = turn(bk(p0 + hp // 4)[:, 0, (hp % 4) * P:(hp % 4 + 1) * P],
                                            T1[:, 2 * hp:2 * hp + 2, :].rearrange("p h d -> p (h d)"), hp == 7)
                            act.after(m_tt, pe.now())
                            dst = QT[:, :, b2 * BLK:(b2 + 1) * BLK] if i == 0 else KT[:, :, WIN + b2 * BLK:WIN + (b2 + 1) * BLK]
                            m_ev = fn(dst, bk(p0, 2).rearrange("p a (h n) -> p (a h) n", n=P), ACT.Copy)
                            free[p0] = free[p0 + 1] = m_ev
                            m_kt = m_ev
                            yield
                        pe.after(free[0], free[1])
                        wv = w_qkv[:, 2 * INNER:].rearrange("p (g j d) -> p j g d", g=4, j=4)
                        for w in range(WPB):
                            xw = xb[:, w * WIN:(w + 1) * WIN]
                            for j in range(4):
                                m_v = mm(bk(w // 2)[32 * j:32 * j + 32, 0, (w % 2) * 256:(w % 2 + 1) * 256].rearrange("p (g d) -> p g d", g=4),
                                         xw, wv[:, j], signal=(w == WPB - 1 and j == 3))
                        act.after(m_v)
                        m_v4 = fn(V4[:, 1 + WPB * b2:1 + WPB * (b2 + 1)].rearrange("p w g d -> p (w g d)"),
                                  bk(0, 2).rearrange("p a n -> p (a n)"), ACT.Copy)
                        free[0] = free[1] = m_v4
                        pe.after(free[2], free[3], m_kt)
                        for par in range(2):
                            mm(bk(2 + par)[:, 0, :].rearrange("p (h n) -> p h n", h=8), ident_bf,
                               bc_at(mask_bf[:, 0 if b == 0 else 1, :], 1, 8), True, False)
                        for hp in range(8):
                            for w in range(WPB):
                                for par in range(2):
                                    rows = slice(64 * par, 64 * par + 64)
                                    q0 = b2 * BLK + w * WIN
                                    m_sc = mm(bk(2 + par)[32 * w:32 * w + 32, 0, hp * 64:(hp + 1) * 64], QT[rows, hp, q0:q0 + WIN],
                                              KT[rows, hp, q0:q0 + 2 * WIN], False, True, signal=(hp == 7 and w == 3 and par == 1))
                        dve.after(m_sc)
                        sc = bk(2, 2)
                        m_mx = total(dve, mx.rearrange("p (h u) -> p u h", u=2), sc.rearrange("p u (h n) -> p u h n", h=8), ALU.max)
                        dve.after(m_mx)
                        for par in range(2):
                            m_sub = tt(dve, PR.rearrange("p k (h u) n -> p u h k n", u=2)[:, par],
                                       sc[:, par, :].rearrange("p (h k n) -> p h k n", h=8, k=2),
                                       bc(bc(mx[:, par::2], 2), WIN), ALU.subtract)
                        free[2] = free[3] = m_sub
                        yield
                        act.after(m_sub)
                        m_ex = fn(PR, PR, ACT.Exp)
                        dve.after(m_ex)
                        m_sm = total(dve, mx, PR[:, 0])
                        m_sm2 = total(dve, sm, PR[:, 1])
                        dve.after(m_sm2)
                        m_sm = tt(dve, sm, sm, mx, ALU.add)
                        dve.after(m_sm)
                        m_sm = recip(sm, sm)
                        pool.after(m_sm, m_ex)
                        m_pr = tt(pool, PR, PR, bc(bc_at(sm, 1, 2), WIN), ALU.mult)
                        yield
                        pe.after(m_pr, free[2], free[3])
                        for k in range(2):
                            for g in range(4):
                                m_tp = turn(bk(2 + k)[:, 0, g * P:(g + 1) * P], PR[:, k, 4 * g:4 * g + 4, :].rearrange("p h n -> p (h n)"),
                                            k == 1 and g == 3)
                        act.after(m_tp, pe.now())
                        for k in range(2):
                            m_prt = fn(PT[:, :, 1 - k, b2 * BLK:(b2 + 1) * BLK], bk(2 + k)[:, 0, :].rearrange("p (g n) -> p g n", g=4), ACT.Copy)
                        free[2] = free[3] = m_prt
                        yield
                    pe.after(m_prt, m_v4, m_zero, *free.values())
                    nw = HALF // WIN
                    started = set()
                    for w in range(nw + 1):
                        for g in range(4):
                            for j in range(4):
                                e_, u = divmod(g, 2)
                                rows = slice(32 * j, 32 * j + 32)
                                q0, q1 = max(0, (w - 1) * WIN), min(HALF, (w + 1) * WIN)
                                o = bk(j)[64 * u:64 * u + 64, 0, e_ * HALF + q0:e_ * HALF + q1]
                                if w == 0:
                                    rhs = PT[rows, g, 1, 0:WIN]
                                elif w == nw:
                                    rhs = PT[rows, g, 0, HALF - WIN:HALF]
                                else:
                                    rhs = PT[rows, g].rearrange("p k n -> p (k n)")[:, (w - 1) * WIN:]
                                    rhs = window_pair(PT, rows, g, w)
                                    o = o.rearrange("p (k n) -> p k n", k=2)
                                first = (j, u) not in started
                                started.add((j, u))
                                m_av = mm(o, V4[rows, w, g, :], rhs, first, w == nw, signal=(w == nw and g == 3 and j == 3))
                    m_avd = m_av
                    act.after(m_av, m_woq)
                    ov = OT.rearrange("p (e j) n -> p j e n", e=2)
                    m_o1 = fn(ov[:, 0:2], bk(0, 2).rearrange("p j (e n) -> p j e n", e=2), ACT.Copy)
                    dve.after(m_av, m_woq)
                    m_o2 = copy(dve, ov[:, 2:4], bk(2, 2).rearrange("p j (e n) -> p j e n", e=2))
                    free[0] = free[1] = m_o1
                    free[2] = free[3] = m_o2
                    yield
                    pe.after(m_o1, m_o2, free[0])
                    for i in range(8):
                        m_wo = mm(bk(0)[:, 0, 0:HALF], w_out[:, i, :], OT[:, i, :], i == 0, i == 7, signal=(i == 7))
                    m_woq = m_wo
                    dve.after(m_wo)
                    if half == 0:
                        pass
                    y = bk(0)[:, 0, 0:HALF]
                    t0 = half * HALF
                    r_lo, r_hi = resid[0:64, s, t0:t0 + HALF], resid[64:P, s, t0 + 1:t0 + HALF + 1]
                    if half == 0:
                        m_y0 = copy(dve, SQ.rearrange("p h d -> p (h d)")[:, 0:HALF], y)
                        keep = T1
                        m_y0 = copy(dve, KEEP[i_stream], y)
                        free[0] = m_y0
                    else:
                        dve.after(m_y0)
                        y0 = KEEP[i_stream]
                        tt(dve, resid[0:64, s, 0:HALF], resid[0:64, s, 0:HALF], y0[0:64, :], ALU.add)
                        m_x0 = tt(dve, resid[64:P, s, 1:HALF + 1], resid[64:P, s, 1:HALF + 1], y0[64:P, :], ALU.add)
                        tt(dve, r_lo, r_lo, y[0:64, :], ALU.add)
                        m_x = tt(dve, r_hi, r_hi, y[64:P, :], ALU.add)
                        free[0] = m_x
                    yield
                pe.after(m_x, free[0])
                m_c = mm(bk(0)[:, 0, :], mat["centre"], xs, signal=True)
                act.after(m_c, m_x)
                m_sq = fn(LT[:, 0, :], bk(0)[:, 0, :], ACT.Square)
                pe.after(m_sq, free[1])
                m_v = mm(bk(1)[:, 0, :], mat["mean"], LT[:, 0, :], signal=True)
                dve.after(m_v)
                m_e = ts(dve, LT[:, 1, :], bk(1)[:, 0, :], LN_EPS, ALU.add)
                free[1] = m_e
                yield
                m_r = rstd(LT, m_e, SEQ)
                dve.after(m_r)
                m_xn = tt(dve, XN, bk(0)[:, 0, :], LT[:, 1, :], ALU.mult)
                free[0] = m_xn
                yield
                for half in range(2):
                    xh = XN[:, half * HALF:(half + 1) * HALF]
                    pe.after(m_xn, *free.values())
                    place = lambda i: bk(2 * (i // 3) + i % 3 // 2)[0:FF_TILES[i % 3][1], 0, (i % 3 % 2) * HALF:(i % 3 % 2 + 1) * HALF]
                    m_hs = {}
                    for i in (3, 4, 5, 0, 1, 2):
                        r0, nr = FF_TILES[i % 3]
                        off = (i // 3) * FF + r0
                        m_hs[i] = mm(place(i), w1[:, off:off + nr], xh, signal=True)
                    m_gs = []
                    for j, (r0, nr) in enumerate(FF_TILES):
                        act.after(m_hs[4 if j < 2 else 5], m_h2)
                        m_gs.append(fn(G[0:nr, j, :], place(3 + j), ACT.Gelu, bias=b1c[0:nr, 3 + j:4 + j]))
                    for j, (r0, nr) in enumerate(FF_TILES):
                        dve.after(m_hs[1 if j < 2 else 2], m_gs[j], m_h2)
                        m_hh = stt(H[0:nr, j, :], place(j), b1c[0:nr, j:j + 1], G[0:nr, j, :], ALU.add, ALU.mult)
                    for k in range(4):
                        free[k] = m_hh
                    yield
                    pe.after(m_hh)
                    for j, (r0, nr) in enumerate(FF_TILES):
                        m_h2 = mm(bk(0)[:, 0, 0:HALF], w2[0:nr, j, :], H[0:nr, j, :], j == 0, j == 2, signal=(j == 2))
                    dve.after(m_h2)
                    t0 = half * HALF
                    stt(resid[0:64, s, t0:t0 + HALF], bk(0)[0:64, 0, 0:HALF], b2c[0:64, 0:1], resid[0:64, s, t0:t0 + HALF], ALU.add, ALU.add)
                    m_x = stt(resid[64:P, s, t0 + 1:t0 + HALF + 1], bk(0)[64:P, 0, 0:HALF], b2c[64:P, 0:1],
                              resid[64:P, s, t0 + 1:t0 + HALF + 1], ALU.add, ALU.add)
                    free[0] = m_x
                    yield
                last = [pe.now(), act.now(), dve.now(), pool.now()]
            for k in range(4):
                bank_free[base + k] = free[k]

        KEEP = [arena.take(HALF) for _ in range(2)]
        streams_at = arena.at
        stream_cols = (arena.cols - arena.at) // 2

        def window_pair(PT, rows, g, w):
            flat = PT[rows, g].rearrange("p k n -> p (k n)")
            a0 = (w - 1) * WIN
            step = HALF + WIN
            v = flat[:, a0:a0 + 1]
            ap = [list(x) for x in v.ap]
            return bass.AP(tensor=v.tensor, offset=v.offset, ap=[ap[0], [step, 2], [1, WIN]])

        for ly in range(depth):
            load_layer(ly)
            weave(*[layer_stream(i, ly, range(i, nseq, 2)) for i in range(2)])
            layer_used[:] = [pe.now(), act.now(), dve.now(), pool.now()]

        fin = Arena(arena.t, arena.cols)
        fin.at = streams_at
        x1b = fin.take(nseq, SEQ)
        sp.after(*layer_used)
        sp.after(m_park)
        l_x1 = load("x1", x1b, out, "x1")
        dve.after(l_x1, *layer_used)
        tt(dve, x1b[0:64], x1b[0:64], resid[0:64, :, 0:SEQ], ALU.add)
        m = tt(dve, x1b[64:P], x1b[64:P], resid[64:P, :, 1:SEQ + 1], ALU.add)
        sp.after(m)
        m_out = store(out, x1b)
        sp.after(m_out)

        block = ctx.enter_context(nc.Block())

        @block.sync
        def _(e):
            sp.play(e)

        @block.tensor
        def _(e):
            pe.play(e)

        @block.scalar
        def _(e):
            act.play(e)

        @block.vector
        def _(e):
            dve.play(e)

        @block.gpsimd
        def _(e):
            pool.play(e)


def arrays(inputs):
    names, mats, rope, mask = constants()
    a = {"c_mats": mats, "c_rope": rope, "c_mask": mask}
    a["xT"] = np.ascontiguousarray(np.asarray(inputs["L0_attn_hidden_states"]).transpose(2, 0, 1))
    for n in ("Wq", "Wk", "Wv", "Wg", "Wo", "Wgk", "Wb", "b_b", "A_log", "dt_bias", "g_norm_weight"):
        a[n] = np.asarray(inputs["L0_attn_" + n])
    for n in ("conv_q", "conv_k", "conv_v"):
        a[n + "T"] = np.ascontiguousarray(np.asarray(inputs["L0_attn_" + n]).T)
    for n in ("Wqkv", "q_scale", "k_scale", "ln_g", "ln_b", "W1", "b1", "W2", "b2"):
        a[n] = np.asarray(inputs["L0_ffn_" + n])
    a["Wo2"] = np.asarray(inputs["L0_ffn_Wo"])
    return names, {k: np.ascontiguousarray(v) for k, v in a.items()}


def kernel(**inputs):
    import concourse.bacc as bacc
    from concourse.bass_utils import run_bass_kernel_spmd

    names, given = arrays(inputs)
    nc = bacc.Bacc("TRN2", target_bir_lowering=False, num_devices=1)
    dram = {n: nc.dram_tensor("in_" + n, v.shape, F32, kind="ExternalInput").ap() for n, v in given.items()}
    out = nc.dram_tensor("outT", (DIM, NSEQ, SEQ), F32, kind="ExternalOutput").ap()
    build(nc, dram, out, names)
    r = run_bass_kernel_spmd(nc, [{"in_" + n: v for n, v in given.items()}], core_ids=[0])
    return np.ascontiguousarray(r.results[0]["outT"].transpose(1, 2, 0))
```

```python
from contextlib import ExitStack

import numpy as np

import concourse.bass as bass
from concourse import mybir

F32 = mybir.dt.float32
BF16 = mybir.dt.bfloat16
ALU = mybir.AluOpType
ACT = mybir.ActivationFunctionType
AX = mybir.AxisListType.X

P = 128
DIM = 128
NSEQ, SEQ = 8, 512
GH, GDK, GDV, TAPS = 12, 64, 128, 4
CHUNK = 64
NCHUNK = SEQ // CHUNK
GRP = 4
NGRP = GH // GRP
LEVELS = 6
DEPTH, HEADS, DH, WIN = 6, 16, 64, 32
INNER = HEADS * DH
FF = int(DIM * 4 * 2 / 3)
FF_TILES = [(0, 128), (128, 128), (256, FF - 256)]
BLK = 128
NBLK = SEQ // BLK
WPB = BLK // WIN
LN_EPS = 1e-5
L2_EPS = 1e-6
NORM_FLOOR = 1e-12
LN_SCALE = 2.0 ** 20
MASKED = -1e30


def constants():
    i = np.arange(P)
    seq = i // CHUNK
    same = seq[:, None] == seq[None, :]
    row, col = i[:, None], i[None, :]
    c = {}
    c["ident"] = np.eye(P)
    c["centre"] = np.eye(P) - 1.0 / P
    c["mean"] = np.full((P, P), 1.0 / P)
    c["later"] = same & (row > col)
    c["upto"] = same & (row <= col)
    c["before"] = same & (row < col)
    c["seq0"] = np.repeat(seq[:, None] == 0, P, 1)
    c["seq1"] = np.repeat(seq[:, None] == 1, P, 1)
    for lv in range(LEVELS):
        c[f"level{lv}"] = (row >> (lv + 1) == col >> (lv + 1)) & ((col >> lv) & 1 == 1) & ((row >> lv) & 1 == 0)
    names = list(c)
    mats = np.stack([np.asarray(c[n], np.float32) for n in names], 1)
    half = np.arange(0, DH, 2, dtype=np.float32)
    inv_freq = (np.float32(1.0) / np.float32(10000.0) ** (half / np.float32(DH))).astype(np.float32)
    t = np.arange(SEQ, dtype=np.float32)
    freqs = (t[:, None] * inv_freq[None, :]).astype(np.float32)
    base = ((half + np.float32(0.4 * DH)) / np.float32(1.4 * DH)).astype(np.float32)
    power = (t - SEQ // 2) / np.float32(WIN // 2)
    scale = (base[None, :] ** power[:, None]).astype(np.float32)
    inv = np.float32(1.0) / scale
    cos, sin = np.cos(freqs), np.sin(freqs)
    rope = np.stack([np.concatenate([cos * scale, cos * scale], 1) * 8, np.concatenate([-sin * scale, sin * scale], 1) * 8,
                     np.concatenate([cos * inv, cos * inv], 1), np.concatenate([-sin * inv, sin * inv], 1)])
    rope = rope.reshape(4, NBLK, P, DH).transpose(2, 0, 1, 3).astype(np.float32)
    q = i % WIN
    j = np.arange(2 * WIN)
    ok = (j[None, :] >= q[:, None]) & (j[None, :] <= q[:, None] + WIN)
    first = ok & ~((i[:, None] < WIN) & (j[None, :] < WIN))
    mask = np.stack([np.where(first, 0, MASKED), np.where(ok, 0, MASKED)], 1).astype(np.float32)
    return names, mats, rope, mask


class Mark:

    def __init__(self, lane, value):
        self.lane, self.value = lane, value


class Lane:

    def __init__(self, sem, step=1):
        self.sem, self.step, self.count, self.queue, self.seen = sem, step, 0, [], {}

    def after(self, *marks):
        for m in marks:
            if m is not None and self.seen.get(id(m.lane), 0) < m.value:
                self.seen[id(m.lane)] = m.value
                self.queue.append(lambda e, m=m: e.wait_ge(m.lane.sem, m.value))

    def do(self, emit, signal=True):
        if not signal:
            self.queue.append(emit)
            return None
        self.count += self.step
        self.queue.append(lambda e: emit(e).then_inc(self.sem, self.step))
        return Mark(self, self.count)

    def now(self):
        return Mark(self, self.count)

    def play(self, engine):
        for emit in self.queue:
            emit(engine)


def weave(*streams):
    live = list(streams)
    while live:
        for s in list(live):
            try:
                next(s)
            except StopIteration:
                live.remove(s)


class Arena:

    def __init__(self, tensor, cols):
        self.t, self.cols, self.at = tensor, cols, 0

    def take(self, *shape):
        n = int(np.prod(shape))
        assert self.at + n <= self.cols, (self.at, n, self.cols)
        v = self.t[:, self.at:self.at + n]
        self.at += n
        if len(shape) == 1:
            return v
        names = "abcd"[:len(shape)]
        return v.rearrange(f"p ({' '.join(names)}) -> p {' '.join(names)}", **dict(zip(names, shape)))


def build(nc, dram, out, names, nseq=NSEQ, depth=DEPTH):
    ctx = ExitStack()
    with ctx:
        def sem(name):
            return ctx.enter_context(nc.semaphore(name))

        pe, act, dve, pool = Lane(sem("s_pe")), Lane(sem("s_act")), Lane(sem("s_dve")), Lane(sem("s_pool"))
        sp = Lane(sem("s_sp"), 16)
        loads = {}

        def load(dst, src, key):
            if key not in loads:
                loads[key] = Lane(sem("s_load_" + key), 16)
            lane = loads[key]
            lane.count += 16
            sp.queue.append(lambda e: e.dma_start(dst, src).then_inc(lane.sem, 16))
            return Mark(lane, lane.count)

        cols = 52900
        arena = Arena(ctx.enter_context(nc.sbuf_tensor("arena", [P, cols], F32)), cols)
        bf = ctx.enter_context(nc.sbuf_tensor("bf", [P, 2 * 64 + P], BF16))
        psum = ctx.enter_context(nc.psum_tensor("banks", [P, 8, 512], F32))

        def mm(o, lhsT, rhs, start=True, stop=True, signal=False):
            return pe.do(lambda e: e.matmul(o, lhsT, rhs, start=start, stop=stop, skip_group_check=True), signal)

        def turn(o, i, signal=False):
            n = i.shape[0]
            return pe.do(lambda e: e.transpose(o, i, mat["ident"][0:n, 0:n]), signal)

        def tt(lane, o, a, b, op):
            return lane.do(lambda e: e.tensor_tensor(o, a, b, op))

        def ts(lane, o, a, s1, op0, s2=None, op1=ALU.bypass):
            return lane.do(lambda e: e.tensor_scalar(o, a, s1, s2, op0, op1))

        def stt(o, a, s, b, op0, op1):
            return dve.do(lambda e: e.scalar_tensor_tensor(out=o, in0=a, scalar=s, in1=b, op0=op0, op1=op1))

        def fn(o, a, f, **kw):
            return act.do(lambda e: e.activation(o, a, f, **kw))

        table_set = [None]

        def tables(name):
            if table_set[0] != name:
                table_set[0] = name
                act.do(lambda e: e.preload_act_table_set(name), False)

        def total(lane, o, a, op=ALU.add, axis=AX):
            return lane.do(lambda e: e.tensor_reduce(o, a, axis, op))

        def memset(lane, o, value):
            return lane.do(lambda e: e.memset(o, value))

        def copy(lane, o, a):
            return lane.do(lambda e: e.tensor_copy(o, a))

        def recip(o, a):
            return dve.do(lambda e: e.reciprocal(o, a))

        def store(o, a):
            return sp.do(lambda e: e.dma_start(o, a))

        def bc(ap, n):
            return ap.unsqueeze(len(ap.shape)).broadcast_to(list(ap.shape) + [n])

        def bc_at(ap, axis, n):
            v = ap.unsqueeze(axis)
            s = list(v.shape)
            s[axis] = n
            return v.broadcast_to(s)

        resid = arena.take(NSEQ, SEQ + 1)[:, 0:nseq]
        mats = arena.take(len(names), P)
        mat = {n: mats[:, i, :] for i, n in enumerate(names)}
        minus_half = arena.take(1)
        base_mark = arena.at
        l_mats = load(mats, dram["c_mats"], "mats")
        m_mh = memset(pool, minus_half, -0.5)

        ntile = nseq // 2 * NCHUNK
        x1 = arena.take(nseq, SEQ)
        xn = arena.take(nseq, SEQ + TAPS - 1)
        w_taps = arena.take(TAPS, NGRP, 4 * 256)
        w_g = arena.take(NGRP, GRP * GDV)
        w_o = arena.take(GH, DIM)
        w_gate = arena.take(2 * GH)
        gate_bias = arena.take(2 * GH)
        one_row = arena.take(P)
        a_log = arena.take(GH)
        g_norm = arena.take(1)
        gk = arena.take(ntile, GH)
        qmul = arena.take(ntile, 2, GH)
        kmul = arena.take(ntile, 4, GH)
        chunk_decay = arena.take(2, ntile, GH // 2)
        l_x = load(x1, dram["xT"], "x")

        l_g = [load(w_g, dram["Wg"].rearrange("c (g n) -> c g n", g=NGRP), "w1"),
               load(w_o, dram["Wo"].rearrange("(h d) n -> d h n", d=GDV), "w1"),
               load(w_gate[:, 0:GH], dram["Wgk"], "w1"),
               load(w_gate[:, GH:2 * GH], dram["Wb"], "w1"),
               load(gate_bias[0:1, 0:GH], dram["dt_bias"].unsqueeze(0), "w1"),
               load(gate_bias[0:1, GH:2 * GH], dram["b_b"].unsqueeze(0), "w1"),
               load(a_log, dram["A_log"].partition_broadcast(P), "w1"),
               load(g_norm, dram["g_norm_weight"].unsqueeze(1), "w1")][-1]

        taps = Arena(arena.t, arena.cols)
        taps.at = arena.at
        conv_rows = taps.take(2, 1536)
        w_raw = taps.take(2, 1536)
        parts = [("Wq", "conv_q", 0, 256), ("Wk", "conv_k", 256, 256), ("Wv", "conv_v", 512, 512)]
        m_tap, n_tap = [None, None], 0
        for wname, cname, off, width in parts:
            n = NGRP * width
            sp.after(*m_tap)
            l_raw = load(w_raw[:, 0, 0:n], dram[wname], "raw")
            for tap in range(TAPS):
                i = n_tap % 2
                sp.after(m_tap[i])
                l_row = load(conv_rows[:, i, 0:n], dram[cname + "T"][tap].partition_broadcast(P), f"row{i}")
                pool.after(l_row, l_raw)
                m_tap[i] = tt(pool, w_taps[:, tap, :, off:off + width], w_raw[:, 0, 0:n].rearrange("p (g n) -> p g n", g=NGRP),
                              conv_rows[:, i, 0:n].rearrange("p (g n) -> p g n", g=NGRP), ALU.mult)
                n_tap += 1
        pool.after(l_g)
        m_wo = ts(pool, w_o, w_o, g_norm[:, 0:1], ALU.mult)
        m_one = memset(pool, one_row, 1.0)
        m_pad = memset(pool, xn[:, :, 0:TAPS - 1], 0.0)

        ln_tmp = taps.take(2, 2, SEQ)
        bank_free = [None] * 8

        def centred(src, banks, tmp, tmp_free, more=()):
            bc_, bv = banks
            pe.after(bank_free[bc_], l_mats, *more)
            m_c = mm(psum[:, bc_, :], mat["centre"], src, signal=True)
            act.after(m_c, tmp_free)
            m_sq = fn(tmp[:, 0, :], psum[:, bc_, :], ACT.Square)
            pe.after(m_sq, bank_free[bv])
            m_v = mm(psum[:, bv, :], mat["mean"], tmp[:, 0, :], signal=True)
            dve.after(m_v, tmp_free)
            m_e = ts(dve, tmp[:, 1, :], psum[:, bv, :], LN_EPS, ALU.add)
            bank_free[bv] = m_e
            return m_e

        def rsqrt_small(o, a, after, eps, scale=1.0):
            pool.after(m_mh, *after)
            m = ts(pool, o, a, scale, ALU.mult, eps, ALU.add)
            pool.after(m)
            return tt(pool, o, o, minus_half[:, 0:1].broadcast_to(list(o.shape)), ALU.pow)

        def rstd(tmp, m_e):
            act.after(m_e)
            m_r = fn(tmp[:, 1, :], tmp[:, 1, :], ACT.Sqrt)
            dve.after(m_r)
            return recip(tmp[:, 1, :], tmp[:, 1, :])

        tmp_free = [None, None]
        m_xn = []
        for s in range(nseq):
            i = s % 2
            m_e = centred(x1[:, s, :], (2 * i, 2 * i + 1), ln_tmp[:, i], tmp_free[i], (l_x,))
            m_r = rstd(ln_tmp[:, i], m_e)
            dve.after(m_r)
            m = tt(dve, xn[:, s, TAPS - 1:], psum[:, 2 * i, :], ln_tmp[:, i, 1, :], ALU.mult)
            bank_free[2 * i] = m
            tmp_free[i] = m
            m_xn.append(m)

        gates = taps.take(ntile, 2 * GH)
        gabs = taps.take(ntile, GH)
        gb = psum[:, 4:6, :]
        pe.after(l_g, m_one, m_xn[-1])
        per = 512 // (2 * GH)
        assert ntile <= 2 * per
        for t in range(ntile):
            pr, c = divmod(t, NCHUNK)
            o = gb[:, t // per, (t % per) * 2 * GH:(t % per + 1) * 2 * GH]
            mm(o, one_row[0:1, :], gate_bias[0:1, :], True, False)
            for q in range(2):
                m_g = mm(o[64 * q:64 * q + 64, :], xn[:, 2 * pr + q, TAPS - 1 + c * CHUNK:TAPS - 1 + (c + 1) * CHUNK], w_gate, False, q == 1,
                         signal=(t == ntile - 1 and q == 1))
        dve.after(m_g)
        n0 = min(per, ntile)
        m = copy(dve, gates[:, 0:n0, :], gb[:, 0, 0:n0 * 2 * GH].rearrange("p (t g) -> p t g", g=2 * GH))
        if ntile > n0:
            m = copy(dve, gates[:, n0:ntile, :], gb[:, 1, 0:(ntile - n0) * 2 * GH].rearrange("p (t g) -> p t g", g=2 * GH))
        bank_free[4] = bank_free[5] = m
        z, beta_in = gates[:, :, 0:GH], gates[:, :, GH:2 * GH]
        beta = kmul[:, :, 1, :]
        act.after(m)
        m_b = fn(beta, beta_in, ACT.Sigmoid)
        m = fn(gabs, z, ACT.Abs)
        act.after(m)
        m = fn(gabs, gabs, ACT.Exp, scale=-1.0)
        act.after(l_g)
        m_a = fn(a_log, a_log, ACT.Exp)
        act.after(m)
        m = fn(gabs, gabs, ACT.Ln, bias=1.0)
        dve.after(m, m_a)
        m = stt(gabs, z, 0.0, gabs, ALU.max, ALU.add)
        dve.after(m)
        m_gk = stt(gk, gabs, -1.0, bc_at(a_log, 1, ntile), ALU.mult, ALU.mult)
        pe.after(m_gk, bank_free[4], bank_free[5], l_mats, *[bank_free[k] for k in range(8)])
        gk_all = gk.rearrange("p t h -> p (t h)")
        ng = ntile * GH
        mm(psum[:, 4, 0:ng], mat["upto"], gk_all)
        mm(psum[:, 5, 0:ng], mat["later"], gk_all)
        mm(psum[:, 6, 0:ng], mat["seq0"], gk_all)
        m_cum = mm(psum[:, 7, 0:ng], mat["seq1"], gk_all, signal=True)
        act.after(m_cum)
        bank = lambda b: psum[:, b, 0:ng].rearrange("p (t h) -> p t h", h=GH)
        eg, tail = qmul[:, :, 1, :], kmul[:, :, 3, :]
        m_eg = fn(eg, bank(4), ACT.Exp)
        m_tail = fn(tail, bank(5), ACT.Exp)
        for q in range(2):
            for par in range(2):
                src = psum[64 * par:64 * par + 64, 6 + q, 0:ng].rearrange("p (t h u) -> p t h u", u=2, h=GH // 2)[:, :, :, par]
                m_dec = fn(chunk_decay[64 * par:64 * par + 64, q], src, ACT.Exp)
        for b in range(4, 8):
            bank_free[b] = m_dec
        pool.after(m_eg, m_b)
        m = tt(pool, kmul[:, :, 2, :], beta, eg, ALU.mult)
        pool.after(m)
        m = ts(pool, qmul[:, :, 1, :], eg, GDK ** -0.5, ALU.mult)
        m = memset(pool, qmul[:, :, 0, :], GDK ** -0.5)
        m_mul = memset(pool, kmul[:, :, 0, :], 1.0)
        x1_mark = [m_xn[-1]]
        setup_done = [pool.now(), act.now(), dve.now(), pe.now()]
        for lane in (pe, act, dve, pool):
            lane.after(*[mk for mk in setup_done if mk.lane is not lane])
            if lane is not pe:
                lane.after(lane.now())

        resid_cols = NSEQ * (SEQ + 1)
        stream_cols = 7600

        def shifted(pr, c):
            v = xn[:, 2 * pr, c * CHUNK:c * CHUNK + 1]
            return bass.AP(tensor=v.tensor, offset=v.offset, ap=[list(v.ap[0]), [1, TAPS], [SEQ + TAPS - 1, 2], [1, CHUNK]])

        def delta_stream(grp):
            a = Arena(arena.t, resid_cols if grp == NGRP - 1 else arena.cols)
            a.at = 0 if grp == NGRP - 1 else arena.at + grp * stream_cols
            QK = a.take(2, GRP, GDK)
            V = a.take(GRP, GDV)
            SG = a.take(GRP, GDV)
            KV4 = a.take(4, GRP, GDK)
            QV2 = a.take(2, GRP, GDK)
            DT = a.take(GRP, P)
            PT = a.take(GRP, P)
            if grp == NGRP - 1:
                a = Arena(arena.t, arena.cols)
                a.at = arena.at + grp * stream_cols
            M = a.take(GRP, P)
            Y = a.take(GRP, P)
            RHS = a.take(GRP, GDV)
            CT = a.take(5, 2, P)
            S = a.take(2, 2, GDV)
            ss = a.take(2, GRP)
            so = a.take(GRP)
            cq = a.take(2, GRP)
            ck = a.take(4, GRP)
            matrix = lambda v: v.rearrange("p a h d -> p (a h d)").rearrange("p (r n) -> p r n", r=GRP)
            XT = PT
            NT = matrix(QK)
            T = matrix(KV4[:, 0:2])
            R = matrix(QV2)
            U = DT
            A, B = 2 * grp, 2 * grp + 1
            AB = psum[:, A:A + 2, :]
            b4 = lambda b: psum[:, b, :].rearrange("p (r n) -> p r n", r=GRP)
            free = {A: bank_free[A], B: bank_free[B]}
            heads = lambda ap, t: ap[:, t, grp * GRP:(grp + 1) * GRP]
            by_parity = lambda ap: ap.rearrange("p (h u) -> p u h", u=2)
            last = []
            for t in range(ntile):
                pr, c = divmod(t, NCHUNK)
                tok = lambda tap: XT[:, tap, :]
                for lane in (pe, act, dve, pool):
                    lane.after(*last)
                if c == 0:
                    m_S = memset(pool, S, 0.0)
                m_xt = copy(pool, XT.rearrange("p t (q n) -> p t q n", q=2), shifted(pr, c))
                pe.after(free[A], m_xt)
                for tap in range(TAPS):
                    m_qk = mm(psum[:, A, :], tok(tap), w_taps[:, tap, grp, 0:512], tap == 0, tap == TAPS - 1, signal=(tap == TAPS - 1))
                pe.after(free[B])
                act.after(m_qk)
                m_qk = fn(QK.rearrange("p a h d -> p (a h d)"), psum[:, A, :], ACT.Silu)
                free[A] = m_qk
                yield
                for tap in range(TAPS):
                    m_v = mm(psum[:, B, :], tok(tap), w_taps[:, tap, grp, 512:1024], tap == 0, tap == TAPS - 1, signal=(tap == TAPS - 1))
                m_ug = tt(pool, Y.rearrange("p (u h) n -> p u h n", u=2),
                          bc_at(bc_at(mat["later"], 1, 2), 1, 2), bc(by_parity(heads(gk, t)), P), ALU.mult)
                act.after(m_v)
                m_v = fn(V.rearrange("p h d -> p (h d)"), psum[:, B, :], ACT.Silu)
                free[B] = m_v
                pe.after(free[A])
                m_g = mm(psum[:, A, :], tok(TAPS - 1), w_g[:, grp, :], signal=True)
                act.after(m_g)
                m_sg = fn(SG.rearrange("p h d -> p (h d)"), psum[:, A, :], ACT.Silu)
                free[A] = m_sg
                pool.after(m_qk)
                m_sq = tt(pool, RHS.rearrange("p h d -> p (h d)"), QK.rearrange("p a h d -> p (a h d)"),
                          QK.rearrange("p a h d -> p (a h d)"), ALU.mult)
                pe.after(m_ug, free[B])
                for r in range(GRP):
                    m_dt = mm(b4(B)[:, r, :], Y[:, r, :], mat["upto"], signal=(r == GRP - 1))
                act.after(m_dt)
                m_dt = fn(DT, b4(B), ACT.Exp)
                free[B] = m_dt
                dve.after(m_sq)
                m_ss = total(dve, ss.rearrange("p a h -> p (a h)"), RHS.rearrange("p h d -> p (h d)").rearrange("p (x d) -> p x d", d=GDK))
                m_rn = rsqrt_small(ss.rearrange("p a h -> p (a h)"), ss.rearrange("p a h -> p (a h)"), (m_ss,), L2_EPS)
                pool.after(m_rn)
                m1 = tt(pool, cq, bc_at(ss[:, 0, :], 1, 2), qmul[:, t, :, grp * GRP:(grp + 1) * GRP], ALU.mult)
                m2 = tt(pool, ck, bc_at(ss[:, 1, :], 1, 4), kmul[:, t, :, grp * GRP:(grp + 1) * GRP], ALU.mult)
                dve.after(m2)
                m_k4 = tt(dve, KV4, bc_at(QK[:, 1], 1, 4), bc(ck, GDK), ALU.mult)
                m_q2 = tt(dve, QV2, bc_at(QK[:, 0], 1, 2), bc(cq, GDK), ALU.mult)
                yield
                pair = lambda v, hp: v[:, 2 * hp:2 * hp + 2, :].rearrange("p h d -> p (h d)")
                pe.after(m_q2, free[A], free[B])
                for f in range(2):
                    for hp in range(2):
                        turn(psum[:, A, (2 * f + hp) * P:(2 * f + hp + 1) * P], pair(KV4[:, f], hp))
                m_ta = turn(psum[:, B, 0:P], pair(QV2[:, 0], 0), True)
                turn(psum[:, B, P:2 * P], pair(QV2[:, 0], 1))
                turn(psum[:, B, 2 * P:3 * P], pair(QV2[:, 1], 0))
                m_tb = turn(psum[:, B, 3 * P:4 * P], pair(QV2[:, 1], 1), True)
                act.after(m_ta)
                m_c1 = fn(CT[:, 0:2].rearrange("p a b c -> p (a b c)"), psum[:, A, :], ACT.Copy)
                act.after(m_tb)
                m_c2 = fn(CT[:, 2:4].rearrange("p a b c -> p (a b c)"), psum[:, B, :], ACT.Copy)
                pe.after(m_c1)
                for hp in range(2):
                    m_tc = turn(psum[:, A, hp * P:(hp + 1) * P], pair(KV4[:, 2], hp), hp == 1)
                act.after(m_tc)
                m_c3 = fn(CT[:, 4].rearrange("p b c -> p (b c)"), psum[:, A, 0:2 * P], ACT.Copy)
                pool.after(m_dt)
                m_m = tt(pool, M, DT, bc_at(mat["before"], 1, GRP), ALU.mult)
                m_dp = tt(pool, DT, DT, bc_at(mat["upto"], 1, GRP), ALU.mult)
                m_vb = tt(pool, V, V, bc(heads(beta, t), GDV), ALU.mult)
                yield
                pe.after(m_c3)
                for par in range(2):
                    for hp in range(2):
                        rows = slice(64 * par, 64 * par + 64)
                        m_np = mm(AB[:, par, hp * 256:(hp + 1) * 256].rearrange("p (k n) -> p k n", k=2),
                                  CT[rows, 0, hp, :], CT[rows, 1:3, hp, :], signal=(par == 1 and hp == 1))
                dve.after(m_np, m_dp)
                prod = AB.rearrange("p u (h k n) -> p u h k n", h=2, k=2)
                m_nt = tt(dve, NT.rearrange("p (u h) n -> p u h n", u=2), prod[:, :, :, 0, :],
                          M.rearrange("p (u h) n -> p u h n", u=2), ALU.mult)
                m_pt = tt(dve, PT.rearrange("p (u h) n -> p u h n", u=2), prod[:, :, :, 1, :],
                          DT.rearrange("p (u h) n -> p u h n", u=2), ALU.mult)
                free[A] = free[B] = m_pt
                yield
                pool.after(m_nt)
                m_M = tt(pool, M, NT, bc_at(mat["level0"], 1, GRP), ALU.mult)
                pe.after(m_M, free[A])
                for r in range(GRP):
                    m_t = turn(b4(A)[:, r, :], M[:, r, :], r == GRP - 1)
                pool.after(m_M)
                m_R = tt(pool, R, bc_at(mat["ident"], 1, GRP), M, ALU.subtract)
                dve.after(m_t)
                m_T = tt(dve, T, bc_at(mat["ident"], 1, GRP), b4(A), ALU.subtract)
                free[A] = m_T
                pe.after(m_R)
                for lv in range(1, LEVELS):
                    pool.after(m_M, m_t, m_R if lv == 1 else None)
                    m_M = tt(pool, M, NT, bc_at(mat[f"level{lv}"], 1, GRP), ALU.mult)
                    pe.after(m_M, m_T, free[A])
                    for r in range(GRP):
                        m_y = mm(b4(A)[:, r, :], M[:, r, :], T[:, r, :], signal=(r == GRP - 1))
                    m_t = m_y
                    act.after(m_y)
                    m_y = fn(Y, b4(A), ACT.Copy)
                    free[A] = m_y
                    yield
                    pe.after(m_y, m_R, free[B])
                    if lv < LEVELS - 1:
                        for r in range(GRP):
                            m_z = mm(b4(B)[:, r, :], R[:, r, :], Y[:, r, :], signal=(r == GRP - 1))
                    for r in range(GRP):
                        m_w = mm(b4(A)[:, r, :], Y[:, r, :], R[:, r, :], signal=(r == GRP - 1))
                    if lv < LEVELS - 1:
                        dve.after(m_z)
                        m_T = tt(dve, T, T, b4(B), ALU.subtract)
                        free[B] = m_T
                    dve.after(m_w)
                    m_R = tt(dve, R, R, b4(A), ALU.subtract)
                    free[A] = m_R
                    yield
                pe.after(m_R, m_S)
                for hp in range(2):
                    for par in range(2):
                        rows = slice(64 * par, 64 * par + 64)
                        for q in range(2):
                            m_ks = mm(AB[64 * q:64 * q + 64, par, hp * GDV:(hp + 1) * GDV], CT[rows, 4, hp, 64 * q:64 * q + 64],
                                      S[rows, q, hp, :], signal=(hp == 1 and par == 1 and q == 1))
                dve.after(m_ks, m_vb)
                m_rhs = tt(dve, RHS.rearrange("p (u h) n -> p u h n", u=2), V.rearrange("p (h u) n -> p u h n", u=2),
                           AB[:, :, 0:2 * GDV].rearrange("p u (h n) -> p u h n", h=2), ALU.subtract)
                yield
                pe.after(m_rhs)
                for r in range(GRP):
                    m_u = mm(b4(A)[:, r, :], R[:, r, :], RHS[:, r, :], signal=(r == GRP - 1))
                act.after(m_u)
                m_u = fn(U, b4(A), ACT.Copy)
                yield
                pe.after(m_u)
                for hp in range(2):
                    for par in range(2):
                        rows = slice(64 * par, 64 * par + 64)
                        o = AB[:, par, hp * GDV:(hp + 1) * GDV]
                        mm(o, PT[:, 2 * par + hp, :], U[:, 2 * par + hp, :], True, False)
                        for q in range(2):
                            m_o = mm(o[64 * q:64 * q + 64, :], CT[rows, 3, hp, 64 * q:64 * q + 64], S[rows, q, hp, :],
                                     False, q == 1, signal=(hp == 1 and par == 1 and q == 1))
                O = AB[:, :, 0:2 * GDV].rearrange("p u (h n) -> p u h n", h=2)
                O2 = AB[:, :, 0:2 * GDV]
                act.after(m_o)
                m_sq = fn(Y.rearrange("p (u h) n -> p u (h n)", u=2), O2, ACT.Square)
                pool.after(m_o)
                m_S = tt(pool, S, S, bc(chunk_decay[:, :, t, grp * 2:grp * 2 + 2], GDV), ALU.mult)
                dve.after(m_sq)
                m_so = total(dve, so, Y)
                m_so = rsqrt_small(so, so, (m_so,), LN_EPS, 1.0 / GDV)
                dve.after(m_so)
                m_on = tt(dve, RHS.rearrange("p (u h) n -> p u h n", u=2), O,
                          bc(so.rearrange("p (u h) -> p u h", u=2), GDV), ALU.mult)
                pool.after(m_on)
                m_on2 = tt(pool, RHS.rearrange("p (u h) n -> p u h n", u=2), RHS.rearrange("p (u h) n -> p u h n", u=2),
                           SG.rearrange("p (h u) n -> p u h n", u=2), ALU.mult)
                yield
                pe.after(m_on)
                for hp in range(2):
                    for q in range(2):
                        rows = slice(64 * q, 64 * q + 64)
                        for par in range(2):
                            m_s = mm(AB[64 * par:64 * par + 64, q, hp * GDV:(hp + 1) * GDV], KV4[rows, 3, 2 * hp + par, :],
                                     U[rows, 2 * par + hp, :], signal=(hp == 1 and par == 1 and q == 1))
                dve.after(m_s, m_S)
                m_S = tt(dve, S, S, AB[:, :, 0:2 * GDV].rearrange("p u (h n) -> p u h n", h=2), ALU.add)
                yield
                pe.after(m_on2, m_S)
                for r in range(GRP):
                    m_ot = turn(b4(A)[:, r, :], RHS[:, r, :], r == GRP - 1)
                act.after(m_ot)
                m_ot = fn(Y, b4(A), ACT.Copy)
                yield
                pe.after(m_ot)
                for r in range(GRP):
                    h = grp * GRP + 2 * (r % 2) + r // 2
                    m_y = mm(psum[:, B, 0:P], w_o[:, h, :], Y[:, r, :], r == 0, r == GRP - 1, signal=(r == GRP - 1))
                dve.after(m_y, x1_mark[0])
                xs = x1[:, 2 * pr:2 * pr + 2, c * CHUNK:(c + 1) * CHUNK]
                m_x = tt(dve, xs, xs, psum[:, B, 0:P].rearrange("p (q n) -> p q n", q=2), ALU.add)
                x1_mark[0] = m_x
                free[A], free[B] = m_ot, m_x
                last = [pe.now(), act.now(), dve.now(), pool.now()]
                yield
            bank_free[A], bank_free[B] = free[A], free[B]

        weave(*[delta_stream(g) for g in range(NGRP)])

        phase_end = [pe.now(), act.now(), dve.now(), pool.now()]
        sp.after(*phase_end)
        m_park = store(out, x1)
        for lane in (pe, act, dve, pool):
            lane.after(*phase_end)

        bank_free[:] = [None] * 8
        lt = Arena(arena.t, arena.cols)
        lt.at = base_mark + nseq * SEQ
        ln_tmp = lt.take(2, 2, SEQ)
        m_z = memset(pool, resid[64:P, :, 0:1], 0.0)
        tmp_free = [None, None]
        for s in range(nseq):
            i = s % 2
            m_e = centred(x1[:, s, :], (2 * i, 2 * i + 1), ln_tmp[:, i], tmp_free[i])
            m_r = rstd(ln_tmp[:, i], m_e)
            dve.after(m_r)
            tt(dve, resid[0:64, s, 0:SEQ], psum[0:64, 2 * i, :], ln_tmp[0:64, i, 1, :], ALU.mult)
            m = tt(dve, resid[64:P, s, 1:SEQ + 1], psum[64:P, 2 * i, :], ln_tmp[64:P, i, 1, :], ALU.mult)
            bank_free[2 * i] = m
            tmp_free[i] = m
        phase_end = [pe.now(), act.now(), dve.now(), pool.now()]
        sp.after(*phase_end)
        sp.after(m_park)
        for lane in (pe, act, dve, pool):
            lane.after(*phase_end)
            lane.after(m_park)

        arena.at = base_mark
        LAYER_BUFS = 2
        rope0 = arena.take(4, NBLK, DH)
        qk_scale = arena.take(2, DH)
        w1_raw = arena.take(2 * FF)
        weights = [{
            "rope": arena.take(4, NBLK, DH),
            "qkv": arena.take(3 * INNER),
            "out": arena.take(8, DIM),
            "w1": arena.take(2 * FF),
            "w2": arena.take(3, DIM),
            "ln": arena.take(2),
            "b1": arena.take(6),
            "b2": arena.take(1),
        } for _ in range(LAYER_BUFS)]
        QK_STREAMS, ATTEND_STREAMS = 4, 2
        SLOTS, V_SLOTS = 2, 3
        QT = arena.take(SLOTS, 8 * BLK)
        KT = arena.take(SLOTS, 8 * (WIN + BLK))
        V2 = arena.take(V_SLOTS, WPB * 8 * DH)
        ATT = arena.take(2, SEQ)
        qk_tmp = [[arena.take(HEADS, DH) for _ in range(3)] for _ in range(QK_STREAMS)]
        back_tmp = [{"PR": arena.take(HEADS, 2 * WIN), "PT": arena.take(8, BLK),
                     "mx": arena.take(HEADS), "sm": arena.take(HEADS)} for _ in range(ATTEND_STREAMS)]
        stats = arena.take(2 * QK_STREAMS, HEADS)
        half_log = arena.take(1)
        LT = arena.take(2, SEQ)
        XN = arena.take(SEQ)
        G = arena.take(3, SEQ)
        qt = lambda n: QT[:, n % SLOTS].rearrange("p (h q) -> p h q", h=8)
        kt = lambda n: KT[:, n % SLOTS].rearrange("p (h q) -> p h q", h=8)
        v2 = lambda n: V2[:, n % V_SLOTS].rearrange("p (w g d) -> p w g d", g=8, d=DH)

        mask_bf = bf[:, 0:128].rearrange("p (k n) -> p k n", k=2)
        ident_bf = bf[:, 128:256]
        mask_f = LT[:, 0, 0:128].rearrange("p (k n) -> p k n", k=2)
        load(rope0, dram["c_rope"], "rope")
        l_rope = load(mask_f, dram["c_mask"], "rope")
        pool.after(l_rope)
        m_maskbf = copy(pool, mask_bf, mask_f)
        memset(pool, half_log, 0.5 * float(np.log(LN_SCALE)))
        m_idbf = copy(pool, ident_bf, mat["ident"])
        for lane in (pe, act, dve, sp):
            lane.after(m_idbf)

        pairs = [[k, ()] for k in range(4)]

        def take_pair():
            k, marks = pairs.pop(0)
            pe.after(*marks)
            return k

        def give_pair(k, *marks):
            pairs.append([k, marks])

        def bank(k, i):
            return psum[:, 2 * k + i, :]

        def both(k):
            return psum[:, 2 * k:2 * k + 2, :]

        nblocks = depth * nseq * NBLK
        where = lambda n: (n // (nseq * NBLK), n // NBLK % nseq, n % NBLK)
        done_q, done_k, done_v, done_scores, done_av = {}, {}, {}, {}, {}
        copied_k = {}
        att_part, done_ffn, ready = {}, {}, {}
        unfinished = {ly: 2 * nseq * NBLK + nseq * NBLK * 2 + nseq for ly in range(depth)}
        used = {}

        def finish(ly):
            unfinished[ly] -= 1
            if unfinished[ly] == 0:
                used[ly] = [pe.now(), act.now(), dve.now(), pool.now()]

        def prepare(ly):
            while ly >= LAYER_BUFS and ly - LAYER_BUFS not in used:
                yield
            before = used.get(ly - LAYER_BUFS, [])
            W = weights[ly % LAYER_BUFS]
            raw_free = ready.get(ly - 1, [])
            sp.after(*before, *raw_free)
            k = f"lw{ly % 2}"
            load(qk_scale[:, 0, :], dram["q_scale"][ly].partition_broadcast(P), k)
            load(qk_scale[:, 1, :], dram["k_scale"][ly].partition_broadcast(P), k)
            load(W["qkv"], dram["Wqkv"][ly], k)
            load(W["out"], dram["Wo2"][ly].rearrange("(g p) n -> p g n", p=P), k)
            load(w1_raw, dram["W1"][ly], k)
            for i, (r0, nr) in enumerate(FF_TILES):
                load(W["w2"][0:nr, i, :], dram["W2"][ly, r0:r0 + nr, :], k)
                load(W["b1"][0:nr, i:i + 1], dram["b1"][ly, r0:r0 + nr].unsqueeze(1), k)
                load(W["b1"][0:nr, 3 + i:4 + i], dram["b1"][ly, FF + r0:FF + r0 + nr].unsqueeze(1), k)
            load(W["b2"], dram["b2"][ly].unsqueeze(1), k)
            load(W["ln"][:, 0:1], dram["ln_g"][ly].unsqueeze(1), k)
            l_w = load(W["ln"][:, 1:2], dram["ln_b"][ly].unsqueeze(1), k)
            yield
            pool.after(l_w, l_rope, *before)
            for i in range(2):
                tt(pool, W["rope"][:, 2 * i], rope0[:, 2 * i], bc_at(qk_scale[:, i, :], 1, NBLK), ALU.mult)
                for z in range(2):
                    lo, hi = slice(32 * z, 32 * z + 32), slice(32 * (1 - z), 32 * (1 - z) + 32)
                    tt(pool, W["rope"][:, 2 * i + 1, :, lo], rope0[:, 2 * i + 1, :, lo], bc_at(qk_scale[:, i, hi], 1, NBLK), ALU.mult)
            m_w1 = ts(pool, W["w1"], w1_raw, W["ln"][:, 0:1], ALU.mult)
            while not pairs:
                yield
            k = take_pair()
            pe.after(l_w)
            for i in range(6):
                r0, nr = FF_TILES[i % 3]
                off = (i // 3) * FF + r0
                m_b = mm(bank(k, 0)[0:nr, i:i + 1], w1_raw[:, off:off + nr], W["ln"][:, 1:2], signal=(i == 5))
            dve.after(m_b, l_w)
            for i in (0, 1, 2):
                nr = FF_TILES[i][1]
                m = tt(dve, W["b1"][0:nr, i:6:3], W["b1"][0:nr, i:6:3], bank(k, 0)[0:nr, i:6:3], ALU.add)
            give_pair(k, m)
            ready[ly] = [m_w1, m, l_w]

        def queries_or_keys(n, i, tmp):
            ly, s, b = where(n)
            x_mark = done_ffn.get((ly - 1, s))
            while ly not in ready or (ly > 0 and x_mark is None) or not pairs or (n >= SLOTS and n - SLOTS not in done_scores) \
                    or (i == 1 and b > 0 and n - 1 not in done_k):
                yield
                x_mark = done_ffn.get((ly - 1, s))
            W = weights[ly % LAYER_BUFS]
            SQ, QN, T1 = qk_tmp[tmp]
            stat, guess = stats[:, tmp, :], stats[:, QK_STREAMS + tmp, :]
            k = take_pair()
            pe.after(*ready[ly], x_mark)
            xb = resid[:, s, b * BLK:(b + 1) * BLK]
            for h in range(2):
                m_p = mm(bank(k, h), xb, W["qkv"][:, i * INNER + h * 512:i * INNER + (h + 1) * 512], signal=(h == 1))
            flat = both(k).rearrange("p a n -> p (a n)")
            act.after(m_p, tmp_free[tmp])
            m_sq = fn(SQ.rearrange("p h d -> p (h d)"), flat, ACT.Square)
            yield
            dve.after(m_sq)
            m_ss = total(dve, stat, SQ)
            dve.after(m_ss)
            m_ss = ts(dve, stat, stat, NORM_FLOOR ** 2, ALU.max)
            yield
            act.after(m_ss)
            tables("natural_log_exp_and_others")
            m_ln = fn(guess, stat, ACT.Ln, scale=LN_SCALE)
            act.after(m_ln)
            m_rn = fn(guess, guess, ACT.Exp, scale=-0.5, bias=half_log)
            yield
            dve.after(m_rn)
            m_n = tt(dve, stat, stat, guess, ALU.mult)
            dve.after(m_n)
            m_n = stt(stat, stat, -0.5, guess, ALU.mult, ALU.mult)
            dve.after(m_n)
            m_rn = stt(stat, stat, 1.5, guess, ALU.add, ALU.mult)
            dve.after(m_rn, tmp_free[tmp])
            m_qn = tt(dve, QN, flat.rearrange("p (h d) -> p h d", d=DH), bc(stat, DH), ALU.mult)
            give_pair(k, m_qn)
            dve.after(m_qn, *ready[ly])
            for z in range(2):
                lo, hi = slice(32 * z, 32 * z + 32), slice(32 * (1 - z), 32 * (1 - z) + 32)
                m_t2 = tt(dve, SQ[:, :, lo], QN[:, :, hi], bc_at(W["rope"][:, 2 * i + 1, b, lo], 1, HEADS), ALU.mult)
            m_t1 = tt(dve, T1, QN, bc_at(W["rope"][:, 2 * i, b, :], 1, HEADS), ALU.mult)
            dve.after(m_t1, m_t2)
            m_t1 = tt(dve, T1, T1, SQ, ALU.add)
            yield
            while not pairs:
                yield
            k = take_pair()
            pe.after(m_t1)
            for hp in range(8):
                m_tt = turn(bank(k, hp // 4)[:, (hp % 4) * P:(hp % 4 + 1) * P],
                            T1[:, 2 * hp:2 * hp + 2, :].rearrange("p h d -> p (h d)"), hp == 7)
            act.after(m_tt, done_scores.get(n - SLOTS), copied_k.get(n - SLOTS + 1))
            dst = qt(n) if i == 0 else kt(n)[:, :, WIN:]
            m_ev = fn(dst, both(k).rearrange("p a (h n) -> p (a h) n", n=P), ACT.Copy)
            give_pair(k, m_ev)
            tmp_free[tmp] = m_tt
            if i == 0:
                done_q[n] = m_ev
            else:
                pool.after(done_k.get(n - 1) if b else None, done_scores.get(n - SLOTS))
                if b:
                    m = copy(pool, kt(n)[:, :, 0:WIN], kt(n - 1)[:, :, BLK:BLK + WIN])
                else:
                    m = memset(pool, kt(n)[:, :, 0:WIN], 0.0)
                copied_k[n] = m
                done_k[n] = m_ev
            finish(ly)
            yield

        def values(n):
            ly, s, b = where(n)
            while ly not in ready or (ly > 0 and (ly - 1, s) not in done_ffn) or len(pairs) < 2 or (n >= V_SLOTS and n - V_SLOTS not in done_av):
                yield
            W = weights[ly % LAYER_BUFS]
            wv = W["qkv"][:, 2 * INNER:].rearrange("p (g u d) -> p u g d", u=2, d=DH)
            if b == 0:
                dve.after(done_av.get(n - V_SLOTS))
                for par in range(2):
                    m_zero = memset(dve, v2(n)[64 * par:64 * par + WIN, 0], 0.0)
            for half in range(2):
                k = take_pair()
                pe.after(*ready[ly], done_ffn.get((ly - 1, s)))
                for w in (2 * half, 2 * half + 1):
                    first = WIN if b == 0 and w == 0 else 0
                    t0 = b * BLK + (w - 1) * WIN
                    for par in range(2):
                        m_v = mm(bank(k, w % 2)[64 * par + first:64 * par + 64].rearrange("p (g d) -> p g d", d=DH),
                                 resid[:, s, t0 + first:t0 + 2 * WIN], wv[:, par], signal=(w % 2 == 1 and par == 1))
                act.after(m_v, done_av.get(n - V_SLOTS))
                if b == 0 and half == 0:
                    for par in range(2):
                        rows = slice(64 * par + WIN, 64 * par + 64)
                        m_ev = fn(v2(n)[rows, 0].rearrange("p g d -> p (g d)"), bank(k, 0)[rows], ACT.Copy)
                    m_ev = fn(v2(n)[:, 1].rearrange("p g d -> p (g d)"), bank(k, 1), ACT.Copy)
                    act.after(m_zero)
                else:
                    m_ev = fn(v2(n)[:, 2 * half:2 * half + 2].rearrange("p w g d -> p (w g d)"), both(k).rearrange("p a n -> p (a n)"), ACT.Copy)
                give_pair(k, m_ev)
            done_v[n] = [m_ev] + ([m_zero] if b == 0 else [])
            finish(ly)
            yield

        def attend(n, tmp):
            ly, s, b = where(n)
            while n not in done_q or n not in done_k or n not in done_v or not pairs \
                    or (b == 0 and att_slot(ly, s) not in att_free):
                yield
            W = weights[ly % LAYER_BUFS]
            B = back_tmp[tmp]
            PR, PT, mx, sm = B["PR"], B["PT"], B["mx"], B["sm"]
            k = take_pair()
            pe.after(done_q[n], done_k[n], copied_k[n], *ready[ly])
            for par in range(2):
                mm(bank(k, par).rearrange("p (h n) -> p h n", h=8), ident_bf,
                   bc_at(mask_bf[:, 0 if b == 0 else 1, :], 1, 8), True, False)
            for hp in range(8):
                for w in range(WPB):
                    for par in range(2):
                        rows = slice(64 * par, 64 * par + 64)
                        m_sc = mm(bank(k, par)[32 * w:32 * w + 32, hp * 64:(hp + 1) * 64], qt(n)[rows, hp, w * WIN:(w + 1) * WIN],
                                  kt(n)[rows, hp, w * WIN:(w + 2) * WIN], False, True, signal=(hp == 7 and w == 3 and par == 1))
            done_scores[n] = m_sc
            dve.after(m_sc, back_free[tmp])
            sc = both(k)
            m_mx = total(dve, mx.rearrange("p (h u) -> p u h", u=2), sc.rearrange("p u (h n) -> p u h n", h=8), ALU.max)
            dve.after(m_mx)
            for par in range(2):
                m_sub = tt(dve, PR.rearrange("p (h u) n -> p u h n", u=2)[:, par],
                           sc[:, par, :].rearrange("p (h n) -> p h n", h=8), bc(mx[:, par::2], 2 * WIN), ALU.subtract)
            give_pair(k, m_sub)
            yield
            act.after(m_sub)
            tables("natural_log_exp_and_others")
            m_ex = fn(PR, PR, ACT.Exp)
            yield
            while not pairs:
                yield
            k = take_pair()
            pe.after(m_ex)
            for g in range(8):
                m_tp = turn(bank(k, g // 4)[:, (g % 4) * BLK:(g % 4 + 1) * BLK], PR[:, 2 * g:2 * g + 2, :].rearrange("p h n -> p (h n)"), g == 7)
            act.after(m_tp, back_free[tmp])
            m_prt = fn(PT, both(k).rearrange("p a (g n) -> p (a g) n", g=4), ACT.Copy)
            give_pair(k, m_prt)
            dve.after(m_ex)
            m_sm = total(dve, sm, PR)
            dve.after(m_sm)
            m_sm = recip(sm, sm)
            yield
            while not pairs:
                yield
            k = take_pair()
            pe.after(m_prt, *done_v[n])
            for g in range(8):
                for w in range(WPB):
                    for par in range(2):
                        rows = slice(64 * par, 64 * par + 64)
                        m_av = mm(bank(k, par)[32 * w:32 * w + 32, g * DH:(g + 1) * DH], PT[rows, g, w * WIN:(w + 1) * WIN],
                                  v2(n)[rows, w, g, :], signal=(g == 7 and w == WPB - 1 and par == 1))
            done_av[n] = m_av
            dve.after(m_av, m_sm)
            for par in range(2):
                m_o = tt(dve, PR.rearrange("p (h u) d -> p u h d", u=2)[:, par], bank(k, par).rearrange("p (h d) -> p h d", h=8),
                         bc(sm[:, par::2], DH), ALU.mult)
            give_pair(k, m_o)
            yield
            while not pairs:
                yield
            k = take_pair()
            pe.after(m_o)
            for g in range(8):
                m_to = turn(bank(k, g // 4)[:, (g % 4) * BLK:(g % 4 + 1) * BLK], PR[:, 2 * g:2 * g + 2, :].rearrange("p h n -> p (h n)"), g == 7)
            act.after(m_to)
            m_ot = fn(PT, both(k).rearrange("p a (g n) -> p (a g) n", g=4), ACT.Copy)
            give_pair(k, m_ot)
            yield
            while not pairs:
                yield
            k = take_pair()
            pe.after(m_ot)
            for i in range(8):
                m_wo = mm(bank(k, 0)[:, 0:BLK], W["out"][:, i, :], PT[:, i, :], i == 0, i == 7, signal=(i == 7))
            back_free[tmp] = m_wo
            slot = att_slot(ly, s)
            act.after(m_wo, att_free[slot])
            m_y = fn(ATT[:, slot, b * BLK:(b + 1) * BLK], bank(k, 0)[:, 0:BLK], ACT.Copy)
            give_pair(k, m_y)
            att_part.setdefault((ly, s), []).append(m_y)
            if len(att_part[ly, s]) == NBLK:
                del att_free[slot]
            finish(ly)
            yield

        def feed_forward(ly, s):
            while len(att_part.get((ly, s), ())) < NBLK:
                yield
            W = weights[ly % LAYER_BUFS]
            slot = att_slot(ly, s)
            xs = resid[:, s, 0:SEQ]
            lo, hi = resid[0:64, s, 0:SEQ], resid[64:P, s, 1:SEQ + 1]
            dve.after(*att_part[ly, s])
            tt(dve, lo, lo, ATT[0:64, slot, :], ALU.add)
            m_x = tt(dve, hi, hi, ATT[64:P, slot, :], ALU.add)
            att_free[slot] = m_x
            yield
            while not pairs:
                yield
            k = take_pair()
            pe.after(m_x)
            m_c = mm(bank(k, 0), mat["centre"], xs, signal=True)
            act.after(m_c, ffn_free[0])
            m_sq = fn(LT[:, 0, :], bank(k, 0), ACT.Square)
            yield
            pe.after(m_sq)
            m_v = mm(bank(k, 1), mat["mean"], LT[:, 0, :], signal=True)
            dve.after(m_v)
            m_e = ts(dve, LT[:, 1, :], bank(k, 1), LN_EPS, ALU.add)
            yield
            act.after(m_e)
            tables("natural_log_exp_and_others")
            m_r = fn(LT[:, 0, :], LT[:, 1, :], ACT.Ln)
            act.after(m_r)
            m_r = fn(LT[:, 0, :], LT[:, 0, :], ACT.Exp, scale=-0.5)
            dve.after(m_r)
            m_r = tt(dve, LT[:, 1, :], LT[:, 1, :], LT[:, 0, :], ALU.mult)
            dve.after(m_r)
            m_r = stt(LT[:, 1, :], LT[:, 1, :], -0.5, LT[:, 0, :], ALU.mult, ALU.mult)
            dve.after(m_r)
            m_r = stt(LT[:, 1, :], LT[:, 1, :], 1.5, LT[:, 0, :], ALU.add, ALU.mult)
            dve.after(m_r, ffn_free[0])
            m_xn = tt(dve, XN, bank(k, 0), LT[:, 1, :], ALU.mult)
            give_pair(k, m_xn)
            yield
            while len(pairs) < 2:
                yield
            k0, k1 = take_pair(), take_pair()
            place = {3: bank(k0, 0), 4: bank(k0, 1), 5: bank(k1, 0), 0: bank(k1, 1)}
            pe.after(m_xn, *ready[ly])

            def first_product(i):
                r0, nr = FF_TILES[i % 3]
                off = (i // 3) * FF + r0
                return mm(place[i][0:nr], W["w1"][:, off:off + nr], XN, signal=True)

            def gated(j, m_a):
                nr = FF_TILES[j][1]
                dve.after(m_a, m_g, *ready[ly])
                return stt(G[0:nr, j, :], place[j][0:nr], W["b1"][0:nr, j:j + 1], G[0:nr, j, :], ALU.add, ALU.mult)

            m_p = [first_product(i) for i in (3, 4, 5, 0)]
            act.after(m_p[2], ffn_free[0], *ready[ly])
            tables("gelu_and_others")
            for j in range(3):
                nr = FF_TILES[j][1]
                m_g = fn(G[0:nr, j, :], place[3 + j][0:nr], ACT.Gelu, bias=W["b1"][0:nr, 3 + j:4 + j])
            m_h = gated(0, m_p[3])
            give_pair(k0, m_g)
            give_pair(k1, m_g, m_h)
            yield
            while not pairs:
                yield
            k = take_pair()
            place[1], place[2] = bank(k, 0), bank(k, 1)
            m_p = [first_product(1), first_product(2)]
            gated(1, m_p[0])
            m_h = gated(2, m_p[1])
            give_pair(k, m_h)
            yield
            while not pairs:
                yield
            k = take_pair()
            pe.after(m_h)
            for j, (r0, nr) in enumerate(FF_TILES):
                m_y = mm(bank(k, 0), W["w2"][0:nr, j, :], G[0:nr, j, :], j == 0, j == 2, signal=(j == 2))
            ffn_free[0] = m_y
            dve.after(m_y)
            stt(lo, bank(k, 0)[0:64], W["b2"][0:64, 0:1], lo, ALU.add, ALU.add)
            m_x = stt(hi, bank(k, 0)[64:P], W["b2"][64:P, 0:1], hi, ALU.add, ALU.add)
            give_pair(k, m_x)
            done_ffn[ly, s] = m_x
            finish(ly)
            yield

        att_slot = lambda ly, s: (ly * nseq + s) % 2
        att_free = {0: None, 1: None}
        tmp_free = [None] * QK_STREAMS
        back_free = [None] * ATTEND_STREAMS
        ffn_free = [None]

        def worker(tasks, number):
            while tasks:
                make = tasks.pop(0)
                yield from make(number)

        qk_tasks = [lambda tmp, n=n, i=i: queries_or_keys(n, i, tmp) for n in range(nblocks) for i in range(2)]
        value_tasks = [lambda _, n=n: values(n) for n in range(nblocks)]
        attend_tasks = [lambda tmp, n=n: attend(n, tmp) for n in range(nblocks)]
        ffn_tasks = [lambda _, ly=ly, s=s: feed_forward(ly, s) for ly in range(depth) for s in range(nseq)]
        layer_tasks = [lambda _, ly=ly: prepare(ly) for ly in range(depth)]
        weave(worker(layer_tasks, 0), worker(ffn_tasks, 0), worker(value_tasks, 0),
              *[worker(attend_tasks, i) for i in range(ATTEND_STREAMS)], *[worker(qk_tasks, i) for i in range(QK_STREAMS)])
        layers_done = [pe.now(), act.now(), dve.now(), pool.now()]

        fin = Arena(arena.t, arena.cols)
        fin.at = base_mark
        x1b = fin.take(nseq, SEQ)
        sp.after(*layers_done)
        sp.after(m_park)
        l_x1 = load(x1b, out, "x1")
        dve.after(l_x1, *layers_done)
        tt(dve, x1b[0:64], x1b[0:64], resid[0:64, :, 0:SEQ], ALU.add)
        m = tt(dve, x1b[64:P], x1b[64:P], resid[64:P, :, 1:SEQ + 1], ALU.add)
        sp.after(m)
        m_out = store(out, x1b)
        sp.after(m_out)

        block = ctx.enter_context(nc.Block())

        @block.sync
        def _(e):
            sp.play(e)

        @block.tensor
        def _(e):
            pe.play(e)

        @block.scalar
        def _(e):
            act.play(e)

        @block.vector
        def _(e):
            dve.play(e)

        @block.gpsimd
        def _(e):
            pool.play(e)


def arrays(inputs):
    names, mats, rope, mask = constants()
    a = {"c_mats": mats, "c_rope": rope, "c_mask": mask}
    a["xT"] = np.ascontiguousarray(np.asarray(inputs["L0_attn_hidden_states"]).transpose(2, 0, 1))
    for n in ("Wq", "Wk", "Wv", "Wg", "Wo", "Wgk", "Wb", "b_b", "A_log", "dt_bias", "g_norm_weight"):
        a[n] = np.asarray(inputs["L0_attn_" + n])
    for n in ("conv_q", "conv_k", "conv_v"):
        a[n + "T"] = np.ascontiguousarray(np.asarray(inputs["L0_attn_" + n]).T)
    for n in ("Wqkv", "q_scale", "k_scale", "ln_g", "ln_b", "W1", "b1", "W2", "b2"):
        a[n] = np.asarray(inputs["L0_ffn_" + n])
    a["Wo2"] = np.asarray(inputs["L0_ffn_Wo"])
    return names, {k: np.ascontiguousarray(v) for k, v in a.items()}


def kernel(**inputs):
    import concourse.bacc as bacc
    from concourse.bass_utils import run_bass_kernel_spmd

    names, given = arrays(inputs)
    nc = bacc.Bacc("TRN2", target_bir_lowering=False, num_devices=1)
    dram = {n: nc.dram_tensor("in_" + n, v.shape, F32, kind="ExternalInput").ap() for n, v in given.items()}
    out = nc.dram_tensor("outT", (DIM, NSEQ, SEQ), F32, kind="ExternalOutput").ap()
    build(nc, dram, out, names)
    r = run_bass_kernel_spmd(nc, [{"in_" + n: v for n, v in given.items()}], core_ids=[0])
    return np.ascontiguousarray(r.results[0]["outT"].transpose(1, 2, 0))
```
